# Optimizing a Trainium2 kernel written in Bass

```python
import numpy as np
import jax
import jax.numpy as jnp

def _softmax(x, axis=-1):
    return jax.nn.softmax(x, axis=axis)

def _gelu(x):
    return jax.nn.gelu(x, approximate=True)

def _silu(x):
    return jax.nn.silu(x)

def _sigmoid(x):
    return jax.nn.sigmoid(x)

def _layernorm(x, axis=-1, eps=1e-05):
    m = jnp.mean(x, axis=axis, keepdims=True)
    v = jnp.var(x, axis=axis, keepdims=True)
    return (x - m) / jnp.sqrt(v + eps)

def _scatter_add(tgt, idx, src, axis=0):
    return tgt.at[idx].add(src)

def _segment_sum(src, seg, n):
    return jax.ops.segment_sum(src, seg, n)
kernel_name = 'mk_adaln_d1_jaxref_r4_9b2dc8'

def setup_inputs(seed: int=0):
    np.random.seed(seed)
    _w = jnp.asarray

    def _L0_attn_setup():
        import jax, jax.numpy as jnp
        import numpy as np
        import math
        H = 512
        B = 4
        T = 512
        LAYERS = 24
        INDEX = 3
        EPS = 1e-05

        def _layer_norm(x, g, b):
            m = jnp.mean(x, axis=-1, keepdims=True)
            v = jnp.mean((x - m) ** 2, axis=-1, keepdims=True)
            return (x - m) * jax.lax.rsqrt(v + EPS) * g + b

        def _time_shift(x):
            return jnp.pad(x, ((0, 0), (1, 0), (0, 0)))[:, :-1, :]

        def _wkv_run(k, v, tm_first, tm_decay):
            C = k.shape[-1]
            aa = jnp.zeros((C,), k.dtype)
            bb = jnp.zeros((C,), k.dtype)
            pp = jnp.full((C,), -1e+38, k.dtype)
            ww = tm_first + k
            p = jnp.maximum(pp, ww)
            e1 = jnp.exp(pp - p)
            e2 = jnp.exp(ww - p)
            a = e1 * aa + e2 * v
            b = e1 * bb + e2
            return a / b
        key = jax.random.key(seed)
        ks = jax.random.split(key, 9)
        i = jnp.arange(H, dtype=jnp.float32)
        r01 = INDEX / (LAYERS - 1)
        r1pz = 1.0 - INDEX / LAYERS
        tm_decay = -5.0 + 8.0 * (i / (H - 1)) ** (0.7 + 1.3 * r01)
        zigzag = ((jnp.arange(H) + 1) % 3 - 1).astype(jnp.float32) * 0.5
        tm_first = jnp.float32(math.log(0.3)) + zigzag
        xr = i / H
        tm_mk = (xr ** r1pz)[None, None, :]
        tm_mv = tm_mk + 0.3 * r01
        tm_mr = (xr ** (0.5 * r1pz))[None, None, :]
        cm_mk = (xr ** r1pz)[None, None, :]
        cm_mr = (xr ** r1pz)[None, None, :]
        s = 1.0 / math.sqrt(H)
        s4 = 1.0 / math.sqrt(4 * H)
        Wk = jax.random.normal(ks[0], (H, H), jnp.float32) * s
        Wv = jax.random.normal(ks[1], (H, H), jnp.float32) * s
        Wr = jax.random.normal(ks[2], (H, H), jnp.float32) * s
        Wo = jax.random.normal(ks[3], (H, H), jnp.float32) * s
        Wkey = jax.random.normal(ks[4], (4 * H, H), jnp.float32) * s
        Wval = jax.random.normal(ks[5], (H, 4 * H), jnp.float32) * s4
        Wcr = jax.random.normal(ks[6], (H, H), jnp.float32) * s
        x = jax.random.normal(ks[7], (B, T, H), jnp.float32)
        return {'x': x, 'ln1_g': jnp.ones((H,), jnp.float32), 'ln1_b': jnp.zeros((H,), jnp.float32), 'ln2_g': jnp.ones((H,), jnp.float32), 'ln2_b': jnp.zeros((H,), jnp.float32), 'tm_decay': tm_decay, 'tm_first': tm_first, 'tm_mk': tm_mk, 'tm_mv': tm_mv, 'tm_mr': tm_mr, 'Wk': Wk, 'Wv': Wv, 'Wr': Wr, 'Wo': Wo, 'cm_mk': cm_mk, 'cm_mr': cm_mr, 'Wkey': Wkey, 'Wval': Wval, 'Wcr': Wcr}
    _L0_attn_in = _L0_attn_setup()

    def _L0_ffn_setup():
        import jax, jax.numpy as jnp
        import numpy as np
        K_TOP = 2
        key = jax.random.key(seed)
        ks = jax.random.split(key, 6)
        s = 0.02
        B, S, H, D = (4, 256, 512, 256)
        E_SH, E_RT = (2, 16)
        return {'x': jax.random.normal(ks[0], (B, S, H), dtype=jnp.float32), 'Wsh_up': jax.random.normal(ks[1], (E_SH, H, D), dtype=jnp.float32) * s, 'Wsh_down': jax.random.normal(ks[2], (E_SH, D, H), dtype=jnp.float32) * s, 'Wrt_up': jax.random.normal(ks[3], (E_RT, H, D), dtype=jnp.float32) * s, 'Wrt_down': jax.random.normal(ks[4], (E_RT, D, H), dtype=jnp.float32) * s, 'W_router': jax.random.normal(ks[5], (H, E_RT), dtype=jnp.float32) * s}
    _L0_ffn_in = _L0_ffn_setup()
    _L0_c = _w((lambda *s: np.random.randn(*s).astype(np.float32) * 0.05)(4, 512))
    _L0_wmod = _w((lambda *s: np.random.randn(*s).astype(np.float32) * 0.05)(512, 6 * 512) * 512 ** (-0.5))
    _d = {'L0_attn_x': _L0_attn_in['x'], 'L0_attn_ln1_g': _L0_attn_in['ln1_g'], 'L0_attn_ln1_b': _L0_attn_in['ln1_b'], 'L0_attn_ln2_g': _L0_attn_in['ln2_g'], 'L0_attn_ln2_b': _L0_attn_in['ln2_b'], 'L0_attn_tm_decay': _L0_attn_in['tm_decay'], 'L0_attn_tm_first': _L0_attn_in['tm_first'], 'L0_attn_tm_mk': _L0_attn_in['tm_mk'], 'L0_attn_tm_mv': _L0_attn_in['tm_mv'], 'L0_attn_tm_mr': _L0_attn_in['tm_mr'], 'L0_attn_Wk': _L0_attn_in['Wk'], 'L0_attn_Wv': _L0_attn_in['Wv'], 'L0_attn_Wr': _L0_attn_in['Wr'], 'L0_attn_Wo': _L0_attn_in['Wo'], 'L0_attn_cm_mk': _L0_attn_in['cm_mk'], 'L0_attn_cm_mr': _L0_attn_in['cm_mr'], 'L0_attn_Wkey': _L0_attn_in['Wkey'], 'L0_attn_Wval': _L0_attn_in['Wval'], 'L0_attn_Wcr': _L0_attn_in['Wcr'], 'L0_ffn_Wsh_up': _L0_ffn_in['Wsh_up'], 'L0_ffn_Wsh_down': _L0_ffn_in['Wsh_down'], 'L0_ffn_Wrt_up': _L0_ffn_in['Wrt_up'], 'L0_ffn_Wrt_down': _L0_ffn_in['Wrt_down'], 'L0_ffn_W_router': _L0_ffn_in['W_router'], 'L0_c': _L0_c, 'L0_wmod': _L0_wmod}
    _x0 = _d['L0_attn_x']
    _d['L0_attn_x'] = jax.random.normal(jax.random.fold_in(jax.random.key(seed), 1), (4, 512, 512), dtype=_x0.dtype)
    del _x0
    return _d

def reference(L0_attn_x, L0_attn_ln1_g, L0_attn_ln1_b, L0_attn_ln2_g, L0_attn_ln2_b, L0_attn_tm_decay, L0_attn_tm_first, L0_attn_tm_mk, L0_attn_tm_mv, L0_attn_tm_mr, L0_attn_Wk, L0_attn_Wv, L0_attn_Wr, L0_attn_Wo, L0_attn_cm_mk, L0_attn_cm_mr, L0_attn_Wkey, L0_attn_Wval, L0_attn_Wcr, L0_ffn_Wsh_up, L0_ffn_Wsh_down, L0_ffn_Wrt_up, L0_ffn_Wrt_down, L0_ffn_W_router, L0_c, L0_wmod):

    def _L0_attn_ref(x, ln1_g, ln1_b, ln2_g, ln2_b, tm_decay, tm_first, tm_mk, tm_mv, tm_mr, Wk, Wv, Wr, Wo, cm_mk, cm_mr, Wkey, Wval, Wcr):
        import jax, jax.numpy as jnp
        import numpy as np
        import math
        H = 512
        B = 4
        T = 512
        LAYERS = 24
        INDEX = 3
        EPS = 1e-05

        def _layer_norm(x, g, b):
            m = jnp.mean(x, axis=-1, keepdims=True)
            v = jnp.mean((x - m) ** 2, axis=-1, keepdims=True)
            return (x - m) * jax.lax.rsqrt(v + EPS) * g + b

        def _time_shift(x):
            return jnp.pad(x, ((0, 0), (1, 0), (0, 0)))[:, :-1, :]

        def _wkv_run(k, v, tm_first, tm_decay):
            C = k.shape[-1]
            aa = jnp.zeros((C,), k.dtype)
            bb = jnp.zeros((C,), k.dtype)
            pp = jnp.full((C,), -1e+38, k.dtype)
            ww = tm_first + k
            p = jnp.maximum(pp, ww)
            e1 = jnp.exp(pp - p)
            e2 = jnp.exp(ww - p)
            a = e1 * aa + e2 * v
            b = e1 * bb + e2
            return a / b
        h = _layer_norm(x, ln1_g, ln1_b)
        hh = _time_shift(h)
        k = (h * tm_mk + hh * (1 - tm_mk)) @ Wk.T
        v = (h * tm_mv + hh * (1 - tm_mv)) @ Wv.T
        r = (h * tm_mr + hh * (1 - tm_mr)) @ Wr.T
        wkv = _wkv_run(k, v, tm_first, tm_decay)
        x = x + jax.nn.sigmoid(r) * wkv @ Wo.T
        h = _layer_norm(x, ln2_g, ln2_b)
        hh = _time_shift(h)
        kk = (h * cm_mk + hh * (1 - cm_mk)) @ Wkey.T
        kv = jax.nn.silu(kk) @ Wval.T
        sr = jax.nn.sigmoid((h * cm_mr + hh * (1 - cm_mr)) @ Wcr.T)
        x = x + sr * kv
        return x

    def _L0_ffn_ref(x, Wsh_up, Wsh_down, Wrt_up, Wrt_down, W_router):
        import jax, jax.numpy as jnp
        import numpy as np
        K_TOP = 2
        B, S, H = x.shape
        E_rt = Wrt_up.shape[0]
        xt = x.reshape(B * S, H)
        sh_mid = jax.nn.gelu(jnp.einsum('th,ehd->ted', xt, Wsh_up), approximate=False)
        shared_out = jnp.einsum('ted,edh->th', sh_mid, Wsh_down)
        probs = jax.nn.softmax(xt @ W_router, axis=-1)
        top_v, top_i = jax.lax.top_k(probs, K_TOP)
        gate = jnp.sum(jax.nn.one_hot(top_i, E_rt, dtype=xt.dtype) * top_v[..., None], axis=1)
        rt_mid = jax.nn.gelu(jnp.einsum('th,ehd->ted', xt, Wrt_up), approximate=False)
        routed_out = jnp.einsum('ted,edh->th', rt_mid * gate[:, :, None], Wrt_down)
        return (shared_out + routed_out).reshape(B, S, H)
    x = L0_attn_x
    mod = (_silu(L0_c) @ L0_wmod).reshape(L0_c.shape[0], 6, 1, -1)
    sa, ca, ga, sb, cb, gb = (mod[:, 0], mod[:, 1], mod[:, 2], mod[:, 3], mod[:, 4], mod[:, 5])
    ga = (2 * (ga >= 0) - 1) * jnp.maximum(jnp.abs(ga), 0.25)
    gb = (2 * (gb >= 0) - 1) * jnp.maximum(jnp.abs(gb), 0.25)
    h = _layernorm(x, axis=-1) * (1 + ca) + sa
    x = x + ga * _L0_attn_ref(h, L0_attn_ln1_g, L0_attn_ln1_b, L0_attn_ln2_g, L0_attn_ln2_b, L0_attn_tm_decay, L0_attn_tm_first, L0_attn_tm_mk, L0_attn_tm_mv, L0_attn_tm_mr, L0_attn_Wk, L0_attn_Wv, L0_attn_Wr, L0_attn_Wo, L0_attn_cm_mk, L0_attn_cm_mr, L0_attn_Wkey, L0_attn_Wval, L0_attn_Wcr)
    h = _layernorm(x, axis=-1) * (1 + cb) + sb
    x = x + gb * _L0_ffn_ref(h, L0_ffn_Wsh_up, L0_ffn_Wsh_down, L0_ffn_Wrt_up, L0_ffn_Wrt_down, L0_ffn_W_router)
    return x

_drawn_inputs = setup_inputs


def setup_inputs(seed=0):
    import zlib

    import numpy as np

    out = dict(_drawn_inputs(seed))
    spreads = {'L0_attn_ln1_g': (1.0, 0.6),
     'L0_attn_ln1_b': (0.0, 0.637),
     'L0_attn_ln2_g': (1.0, 0.6),
     'L0_attn_ln2_b': (0.0, 0.8)}
    factors = {'L0_attn_tm_mr': 3.006,
     'L0_attn_cm_mr': 4.68,
     'L0_ffn_Wrt_up': 8.0,
     'L0_ffn_Wrt_down': 8.0,
     'L0_ffn_W_router': 8.0,
     'L0_ffn_Wsh_up': 3.254,
     'L0_ffn_Wsh_down': 3.118}
    for name, (base, spread) in spreads.items():
        noise = np.random.default_rng([zlib.crc32(name.encode()), seed]).standard_normal(out[name].shape)
        drawn = base * np.exp(spread * noise) if base else spread * noise
        out[name] = jnp.asarray(drawn.astype(out[name].dtype))
    for name, factor in factors.items():
        out[name] = (out[name] * factor).astype(out[name].dtype)
    return out
```

```python
from contextlib import ExitStack

import concourse.bass as bass
from concourse import mybir

F32 = mybir.dt.float32
F32R = mybir.dt.float32r
BF16 = mybir.dt.bfloat16
I32 = mybir.dt.int32
ALU = mybir.AluOpType
ACT = mybir.ActivationFunctionType
AX = mybir.AxisListType

P = 128
H = 512
KT = H // P
NB = 4
T = 512
TT = T // P
NT = NB * TT
F = 4 * H
MF = F // P
EPS = 1e-5
UNIT = KT * H
HALF = UNIT // 2
NE = 16
NS = NB * T * 2 // P + NE
FULL = NB * T * 2 // P
NSX = NS + 3
RING = 7
BASE = 2
PRE = RING - BASE
AHEAD = 2
NSILU = 4
UNIT_SLOT = [0, 1, 2, 3, 7, 4, 5, 6]
PP0 = -1e38

V_MK, V_MV, V_MR, V_CK, V_CR, V_G1, V_B1, V_G2, V_B2, V_FIRST = range(10)


class Count:

    def __init__(self, sem, step=1):
        self.sem, self.step, self.n = sem, step, 0

    def up(self, ins):
        self.n += 1
        ins.then_inc(self.sem, self.step)
        return self.n


def adaln_block(nc, x_d, c_d, wmod_d, vecs_d, wtm_d, wcm_d, wrt_d, wex_d, out_d):
    top = ExitStack()
    with top:
        def sem(name):
            return top.enter_context(nc.semaphore(name))

        def sbuf(stack, name, shape, dt=F32):
            return stack.enter_context(nc.sbuf_tensor(name, shape, dt))

        def psum(stack, name, shape, dt=F32):
            return stack.enter_context(nc.psum_tensor(name, shape, dt))

        mod_s = nc.dram_tensor("mod_s", (6, NB, H), F32).ap()
        h0_s = nc.dram_tensor("h0_s", (NT, P, H), F32).ap()
        x2_s = nc.dram_tensor("x2_s", (NT, P, H), F32).ap()
        x4_s = nc.dram_tensor("x4_s", (NT, P, H), F32).ap()
        h5_s = nc.dram_tensor("h5_s", (NT, P, H), F32).ap()
        h5T_s = nc.dram_tensor("h5T_s", (NB, P, KT, T), F32).ap()
        base_s = nc.dram_tensor("base_s", (NT, P, H), F32).ap()
        xs_s = nc.dram_tensor("xs_s", (NSX * P, H), F32).ap()
        ys_s = nc.dram_tensor("ys_s", (NSX * P, H), F32).ap()
        sr_s = nc.dram_tensor("sr_s", (NT, P, H), F32).ap()
        xk2_s = nc.dram_tensor("xk2_s", (NB, KT, P, T), F32).ap()

        ident = sbuf(top, "ident", [P, P])
        vecs = sbuf(top, "vecs", [P, 10, KT])
        neghalf = sbuf(top, "neghalf", [P, 1])
        wrt = sbuf(top, "wrt", [P, KT, NE])
        gates = sbuf(top, "gates", [P, 2, NT])
        pos = sbuf(top, "pos", [P, 2, NT], I32)
        tab = sbuf(top, "tab", [1, 2, NSX], I32)
        tend = sbuf(top, "tend", [1, NE + 1], I32)
        zero = sbuf(top, "zero", [P, P])
        rev = sbuf(top, "rev", [P, NE])
        thr = sbuf(top, "thr", [P, NE])
        upper = sbuf(top, "upper", [P, P], BF16)
        onesb = sbuf(top, "onesb", [P, 1], BF16)
        ones16 = sbuf(top, "ones16", [P, 1])
        sidx = sbuf(top, "sidx", [1, NSX])
        iot = sbuf(top, "iot", [P, NSX], I32)
        stage = sbuf(top, "stage", [P, 2, HALF])

        ph1 = ExitStack()
        wkv_w = sbuf(ph1, "wkv_w", [P, 2, 2, KT, H], F32R)
        overlay = ExitStack()
        wmod = sbuf(overlay, "wmod", [P, 6, KT, H])
        overlay.close()
        wro_w = sbuf(ph1, "wro_w", [P, 3, 2, KT, H], F32R)
        mix = sbuf(ph1, "mix", [P, 2, 2, KT, T], F32R)
        overlay = ExitStack()
        modr = sbuf(overlay, "modr", [NB, 6, H])
        modt = sbuf(overlay, "modt", [NB, 2, H])
        overlay.close()
        rw = sbuf(ph1, "rw", [P, 2, KT, T], F32R)
        hT = sbuf(ph1, "hT", [P, KT, T + 1])
        dT = sbuf(ph1, "dT", [P, KT, T])
        eT = sbuf(ph1, "eT", [P, KT, T])
        rec = sbuf(ph1, "rec", [P, 2, T])
        sig = sbuf(ph1, "sig", [P, 2, T])
        raw = sbuf(ph1, "raw", [P, 2, T])
        xb = sbuf(ph1, "xb", [P, TT, H])
        hn = sbuf(ph1, "hn", [P, 2, H])
        h0r = sbuf(ph1, "h0r", [P, 2, H])
        x2b = sbuf(ph1, "x2b", [P, TT, H])
        ca_bc = sbuf(ph1, "ca_bc", [P, H])
        sa_bc = sbuf(ph1, "sa_bc", [P, H])
        st1 = sbuf(ph1, "st1", [P, TT, 6])
        mv1 = sbuf(ph1, "mv1", [P, TT, 2])
        rs1 = sbuf(ph1, "rs1", [P, TT])
        st2 = sbuf(ph1, "st2", [P, TT, 6])
        mv2 = sbuf(ph1, "mv2", [P, TT, 2])
        rs2 = sbuf(ph1, "rs2", [P, TT])
        st3 = sbuf(ph1, "st3", [P, TT, 6])
        mv3 = sbuf(ph1, "mv3", [P, TT, 2])
        rs3 = sbuf(ph1, "rs3", [P, TT])
        cT = sbuf(ph1, "cT", [P, KT, NB])
        sgc = sbuf(ph1, "sgc", [P, KT, NB])
        srb = sbuf(ph1, "srb", [P, 2, H])
        ps1 = ExitStack()
        mm_ps = [psum(ps1, f"mm_ps{i}", [P, 512]) for i in range(4)]
        tp_ps = [psum(ps1, f"tp_ps{i}", [P, KT, P]) for i in range(2)]
        ph1.close()
        ps1.close()

        ph2 = ExitStack()
        cm_w = sbuf(ph2, "cm_w", [P, 8, 2, KT, H], F32R)
        xk = sbuf(ph2, "xk", [P, 2, KT, T], F32R)
        xkr = sbuf(ph2, "xkr", [P, 2, T])
        silu = sbuf(ph2, "silu", [P, NSILU, 2, T], F32R)
        ld = sbuf(ph2, "ld", [P, 2, 2, H])
        bc2 = sbuf(ph2, "bc2", [P, 3, H])
        x4b = sbuf(ph2, "x4b", [P, TT, H])
        h5b = sbuf(ph2, "h5b", [P, 2, H])
        h5T = sbuf(ph2, "h5T", [P, 2, KT, P])
        st5 = sbuf(ph2, "st5", [P, 2, 6])
        mv5 = sbuf(ph2, "mv5", [P, 2, 2])
        rs5 = sbuf(ph2, "rs5", [P, 2])
        ps2 = ExitStack()
        kk_ps = [psum(ps2, f"kk_ps{i}", [P, 512]) for i in range(2)]
        kv_ps = [psum(ps2, f"kv_ps{i}", [P, 512]) for i in range(4)]
        t5_ps = psum(ps2, "t5_ps", [P, KT, P])
        rt_ps = psum(ps2, "rt_ps", [P, NT, NE])
        ph2.close()
        ps2.close()

        ph3 = ExitStack()
        ex_w = sbuf(ph3, "ex_w", [P, RING, 2, UNIT], F32R)
        ht = sbuf(ph3, "ht", [P, 2, KT, T], F32R)
        h5r = sbuf(ph3, "h5r", [P, 2, T])
        mid = sbuf(ph3, "mid", [P, 2, 2, KT, T], F32R)
        yb = sbuf(ph3, "yb", [P, 2, H])
        x4l = sbuf(ph3, "x4l", [P, 2, H])
        gb_bc = sbuf(ph3, "gb_bc", [P, H])
        h5l = sbuf(ph3, "h5l", [P, 4, H])
        lg = sbuf(ph3, "lg", [P, NT, NE])
        pr = sbuf(ph3, "pr", [P, NT, NE])
        oh = sbuf(ph3, "oh", [P, 2, NT, NE])
        tmp = sbuf(ph3, "tmp", [P, NT, NE])
        red = sbuf(ph3, "red", [P, NT])
        red2 = sbuf(ph3, "red2", [P, NT])
        chosen = sbuf(ph3, "chosen", [P, NT, NE], BF16)
        off = sbuf(ph3, "off", [P, NT + 1, NE])
        ntile = sbuf(ph3, "ntile", [P, NE])
        tends = sbuf(ph3, "tends", [P, NE])
        cmp = sbuf(ph3, "cmp", [1, NSX, NE])
        tabf = sbuf(ph3, "tabf", [1, 4, NSX])
        ps3 = ExitStack()
        up_ps = [psum(ps3, f"up_ps{i}", [P, 512]) for i in range(2)]
        dn_ps = [psum(ps3, f"dn_ps{i}", [P, 512]) for i in range(3)]
        pf_ps = psum(ps3, "pf_ps", [P, 2, NT, NE])
        ph3.close()
        ps3.close()

        ph4 = ExitStack()
        ex_w4 = sbuf(ph4, "ex_w4", [P, RING, 2, UNIT], F32R)
        xsb = sbuf(ph4, "xsb", [P, 2, H])
        xsT = sbuf(ph4, "xsT", [P, 2, 2, KT, P], F32R)
        mb = sbuf(ph4, "mb", [P, 2, H // 2])
        mbT = sbuf(ph4, "mbT", [P, 2, 2, 2, P], F32R)
        ysb = sbuf(ph4, "ysb", [P, 2, H])
        g1b = sbuf(ph4, "g1b", [P, 4, H])
        g2b = sbuf(ph4, "g2b", [P, 4, H])
        bsb = sbuf(ph4, "bsb", [P, 4, H])
        gb2 = sbuf(ph4, "gb2", [P, NB, H])
        ps4 = ExitStack()
        xs_ps = [psum(ps4, f"xs_ps{i}", [P, KT, P]) for i in range(2)]
        up4_ps = [psum(ps4, f"up4_ps{i}", [P, 512]) for i in range(2)]
        tm_ps = psum(ps4, "tm_ps", [P, KT, P])
        dn4_ps = [psum(ps4, f"dn4_ps{i}", [P, 512]) for i in range(2)]
        ph4.close()
        ps4.close()

        s_const = sem("s_const")
        s_small = sem("s_small")
        s_wmod = [sem(f"s_wmod{i}") for i in range(6)]
        s_csil = sem("s_csil")
        s_modps = sem("s_modps")
        s_modsb = sem("s_modsb")
        s_modst = sem("s_modst")
        s_stage = [sem("s_stage0"), sem("s_stage1")]
        s_whi = sem("s_whi")
        s_wlo = sem("s_wlo")
        s_x = [sem(f"s_xt{i}") for i in range(TT)]
        s_bc = sem("s_bc")
        s_st1 = sem("s_st1")
        s_rs1 = sem("s_rs1")
        s_hca = sem("s_hca")
        s_h0 = sem("s_h0")
        s_h0st = [sem(f"s_h0st{i}") for i in range(TT)]
        s_st2 = sem("s_st2")
        s_rs2 = sem("s_rs2")
        s_hn = sem("s_hn")
        s_tp = sem("s_tp")
        s_hT = sem("s_hT")
        s_dT = sem("s_dT")
        s_raw = sem("s_raw")
        s_mhi = sem("s_mhi")
        s_mlo = sem("s_mlo")
        s_mm = sem("s_mm")
        s_ke = sem("s_ke")
        s_e2 = sem("s_e2")
        s_rec = sem("s_rec")
        s_va = sem("s_va")
        s_sig = sem("s_sig")
        s_rw = sem("s_rw")
        s_rwhi = sem("s_rwhi")
        s_rwlo = sem("s_rwlo")
        s_sr = sem("s_sr")
        s_srst = [sem("s_srst0"), sem("s_srst1")]
        s_h0r = [sem("s_h0r0"), sem("s_h0r1")]
        s_x2 = sem("s_x2")
        s_x2st = [sem(f"s_x2st{i}") for i in range(TT)]
        s_st3 = sem("s_st3")
        s_rs3 = sem("s_rs3")
        s_xkst = [sem("s_xkst0"), sem("s_xkst1")]
        s_dve = sem("s_dve")
        s_con = sem("s_con")
        s_zero = sem("s_zero")
        s_h5r = [sem("s_h5r0"), sem("s_h5r1")]
        s_hthi = sem("s_hthi")
        s_htlo = sem("s_htlo")
        s_up = sem("s_up")
        s_gelu = sem("s_gelu")
        s_midhi = sem("s_midhi")
        s_midlo = sem("s_midlo")
        s_dn = sem("s_dn")
        s_gsh = sem("s_gsh")
        s_base = sem("s_base")
        s_gb = sem("s_gb")
        s_x4l = [sem("s_x4l0"), sem("s_x4l1")]
        s_basest = [sem("s_basest0"), sem("s_basest1")]
        s_sub = sem("s_sub")
        s_exp = sem("s_exp")
        s_cho = sem("s_cho")
        s_pf = sem("s_pf")
        s_pos = sem("s_pos")
        s_h5l = [sem(f"s_h5l{i}") for i in range(4)]
        s_scat = [sem(f"s_scat{i}") for i in range(4)]
        s_exr = sem("s_exr")
        s_exs = [sem("s_exs0"), sem("s_exs1")]
        s_exd = sem("s_exd")
        s_xs = [sem("s_xs0"), sem("s_xs1")]
        s_tx = sem("s_tx")
        s_txhi = sem("s_txhi")
        s_txlo = sem("s_txlo")
        s_u4 = sem("s_u4")
        s_g4 = sem("s_g4")
        s_tm = sem("s_tm")
        s_tmhi = sem("s_tmhi")
        s_tmlo = sem("s_tmlo")
        s_d4 = sem("s_d4")
        s_y4 = sem("s_y4")
        s_yst = [sem("s_yst0"), sem("s_yst1")]
        s_end = sem("s_end")
        s_gb2 = sem("s_gb2")
        s_o1 = sem("s_o1")
        s_o4 = sem("s_o4")
        s_out = [sem(f"s_out{i}") for i in range(4)]
        s_xkr = [sem("s_xkr0"), sem("s_xkr1")]
        s_xkhi = sem("s_xkhi")
        s_xklo = sem("s_xklo")
        s_kk = sem("s_kk")
        s_silu = sem("s_silu")
        s_sihi = sem("s_sihi")
        s_silo = sem("s_silo")
        s_kv = sem("s_kv")
        s_kvr = sem("s_kvr")
        s_ld = [sem("s_ld0"), sem("s_ld1")]
        s_lds = [sem(f"s_lds{i}") for i in range(TT)]
        s_bc2 = sem("s_bc2")
        s_x3 = sem("s_x3")
        s_gx3 = sem("s_gx3")
        s_x4 = sem("s_x4")
        s_st5 = sem("s_st5")
        s_rs5 = sem("s_rs5")
        s_hcb = sem("s_hcb")
        s_h5 = sem("s_h5")
        s_x4st = [sem("s_x4st0"), sem("s_x4st1")]
        s_h5st = [sem("s_h5st0"), sem("s_h5st1")]
        s_t5 = sem("s_t5")
        s_h5T = sem("s_h5T")
        s_h5Tst = [sem("s_h5Tst0"), sem("s_h5Tst1")]
        s_rt = sem("s_rt")
        s_id = sem("s_id")

        order1 = []
        for b in range(NB):
            order1 += [("K", b), ("V", b), ("R", b)]
            if b:
                order1.append(("S", b - 1))
            order1.append(("O", b))
        order1.append(("S", NB - 1))
        turns = [(1, 0)]
        for b in range(NB):
            if b:
                turns.append((2, b - 1))
            if b + 1 < NB:
                turns.append((1, b + 1))
        turns.append((2, NB - 1))
        mixes = []
        for kind, b in turns:
            pass
        mixes = [m for s, b in order1 if s in "KVRS" for m in [(s, b)]]

        def mix_at(s, b):
            return mixes.index((s, b))

        used_by = {"K": s_ke, "V": s_va, "R": s_sig, "S": s_sr, "O": s_x2}
        free_step = {"K": 1, "V": 1, "R": 1, "S": 1, "O": 1}
        raws = []

        block = top.enter_context(nc.Block())

        def mm3(pe, out, lhs, rhs, first, last):
            pe.matmul(out, lhs[0], rhs[0], start=first, stop=False)
            pe.matmul(out, lhs[0], rhs[1], start=False, stop=False)
            return pe.matmul(out, lhs[1], rhs[0], start=False, stop=last)

        w_of = {"K": wkv_w[:, 0], "V": wkv_w[:, 1], "R": wro_w[:, 0], "O": wro_w[:, 1], "S": wro_w[:, 2]}
        w_load_order = ["K", "V", "R", "O", "S"]

        raw_order = [("K", 0), ("V", 0)]
        for b in range(NB):
            raw_order.append(("R", b))
            if b:
                raw_order += [("X", b - 1), ("S", b - 1)]
            if b + 1 < NB:
                raw_order += [("K", b + 1), ("V", b + 1)]
        raw_order += [("X", NB - 1), ("S", NB - 1)]
        split_order = [r for r in raw_order if r[0] != "X"]

        def xk_stored(n):
            return 16 * sum(1 for i in range(n) if i % 2 == (n - 1) % 2 and raw_order[i // KT][0] == "X")

        def cm_half(n):
            n -= 10
            return wcm_d[n // 2, :, (n % 2) * HALF:(n % 2 + 1) * HALF]

        def ex_half(n):
            n -= 26
            return wex_d[n // 2, :, (n % 2) * HALF:(n % 2 + 1) * HALF]

        def ring_slot(e):
            return (BASE + e) % RING

        def ex_free():
            last = (NB - 1) * MF
            return [(s_kk, last + 4), (s_kv, last + 4), (s_kk, last + 8), (s_kv, last + 8),
                    (s_kv, last + 12), (s_kk, last + 16), (s_kv, last + 16)]

        def cm_unit(u):
            return cm_w[:, UNIT_SLOT[u]]

        def cm_free():
            return [mm_count("K", NB - 1, 3), mm_count("V", NB - 1, 3), mm_count("R", NB - 1, 3),
                    mm_count("O", NB - 1, 3), mm_count("O", NB - 1, 3)] + 3 * [mm_count("S", NB - 1, 3)]

        def raw_count(s, b, k):
            return raw_order.index((s, b)) * KT + k + 1

        def split_count(s, b, k):
            return split_order.index((s, b)) * KT + k + 1

        def hn_count(kind, b, j):
            return turns.index((kind, b)) * TT + j + 1

        def hT_count(kind, b):
            return (turns.index((kind, b)) + 1) * TT

        def stage_index(s, b):
            return order1.index((s, b))

        def mm_count(s, b, j):
            return order1.index((s, b)) * 4 + j + 1

        def mix_slot(s, b):
            return split_order.index((s, b)) % 2

        def bank_free(eng, s, b, j):
            i = stage_index(s, b)
            if i == 0:
                return
            s0, b0 = order1[i - 1]
            eng.wait_ge(used_by[s0], b0 * 4 + j + 1)

        @block.sync
        def _(sp):
            sp.dma_start(cT[:, :, :], c_d).then_inc(s_small, 16)
            sp.dma_start(vecs[:, :, :], vecs_d).then_inc(s_small, 16)
            sp.dma_start(wrt[:, :, :], wrt_d).then_inc(s_small, 16)
            for i in (0, 1):
                sp.dma_start(wmod[:, i], wmod_d[i]).then_inc(s_wmod[i], 16)

            nx = [0]

            def load_x(b):
                for j in range(TT):
                    t = b * TT + j
                    if b:
                        sp.wait_ge(s_h0st[j], 16 * b)
                        sp.wait_ge(s_hn, hn_count(1, b - 1, j))
                    sp.dma_start(xb[:, j], x_d[t]).then_inc(s_x[j], 16)

            def load_bc(b):
                if b == 0:
                    sp.wait_ge(s_modst, 32)
                else:
                    sp.wait_ge(s_h0, TT * b)
                sp.dma_start(ca_bc[:, :], mod_s[1, b:b + 1, :].partition_broadcast(P)).then_inc(s_bc, 16)
                sp.dma_start(sa_bc[:, :], mod_s[0, b:b + 1, :].partition_broadcast(P)).then_inc(s_bc, 16)

            def load_half(n, src):
                if n >= 2:
                    sp.wait_ge(s_whi, n - 1)
                    sp.wait_ge(s_wlo, n - 1)
                sp.dma_start(stage[:, n % 2], src).then_inc(s_stage[n % 2], 16)

            def clear_slots(i):
                n = -(-NSX // NB)
                sp.wait_ge(s_con, 1)
                for q in range(i * n, min(NSX, (i + 1) * n)):
                    for rows_s in (xs_s, ys_s):
                        if rows_s is xs_s or q >= FULL:
                            sp.dma_start(rows_s[q * P:(q + 1) * P, :].rearrange("p (k c) -> p k c", k=KT),
                                         zero[:, :].rearrange("p (k c) -> p k c", k=1).to_broadcast([P, KT, P]))\
                                .then_inc(s_zero, 16)

            load_x(0)
            for n in range(4):
                load_half(n, wtm_d[n // 2, :, (n % 2) * HALF:(n % 2 + 1) * HALF])
                if n == 1:
                    sp.wait_ge(s_modsb, 2)
                    for i in (0, 1):
                        sp.dma_start(mod_s[i], modr[:, i]).then_inc(s_modst, 16)
                    load_bc(0)
                    for i in range(2, 6):
                        sp.dma_start(wmod[:, i], wmod_d[i]).then_inc(s_wmod[i], 16)
            sp.wait_ge(s_modps, 6)
            for n in range(4, 10):
                load_half(n, wtm_d[n // 2, :, (n % 2) * HALF:(n % 2 + 1) * HALF])
            sp.wait_ge(s_modsb, 6)
            for i in range(2, 6):
                sp.dma_start(mod_s[i], modr[:, i]).then_inc(s_modst, 16)

            def store_h0(b):
                for j in range(TT):
                    t = b * TT + j
                    sp.wait_ge(s_h0, t + 1)
                    sp.dma_start(h0_s[t], xb[:, j]).then_inc(s_h0st[j], 16)

            def load_h0(b):
                for j in range(TT):
                    t = b * TT + j
                    sp.wait_ge(s_h0st[j], 16 * (b + 1))
                    if t >= 2:
                        sp.wait_ge(s_x2, t - 1)
                    sp.dma_start(h0r[:, t % 2], h0_s[t]).then_inc(s_h0r[t % 2], 16)

            def store_x2(b):
                for j in range(TT):
                    t = b * TT + j
                    sp.wait_ge(s_x2, t + 1)
                    sp.dma_start(x2_s[t], x2b[:, j]).then_inc(s_x2st[j], 16)

            def store_xk(b):
                for k in range(KT):
                    n = b * KT + k
                    sp.wait_ge(s_raw, raw_count("X", b, k))
                    sp.dma_start(xk2_s[b, k], raw[:, (raw_count("X", b, k) - 1) % 2]).then_inc(
                        s_xkst[(raw_count("X", b, k) - 1) % 2], 16)

            def store_sr(b):
                for j in range(TT):
                    t = b * TT + j
                    sp.wait_ge(s_sr, t + 1)
                    sp.dma_start(sr_s[t], srb[:, t % 2]).then_inc(s_srst[t % 2], 16)

            store_h0(0)
            for b in range(NB):
                if b + 1 < NB:
                    load_bc(b + 1)
                    load_x(b + 1)
                    store_h0(b + 1)
                if b:
                    store_xk(b - 1)
                    store_sr(b - 1)
                load_h0(b)
                clear_slots(b)
                store_x2(b)
            for n in range(10, 16):
                load_half(n, cm_half(n))
            store_xk(NB - 1)
            store_sr(NB - 1)
            for n in range(16, 20):
                load_half(n, cm_half(n))
            for j in range(TT):
                sp.wait_ge(s_x2st[j], 16 * NB)
            for j in range(2):
                sp.wait_ge(s_srst[j], 16 * NT // 2)
            for j in range(2):
                sp.wait_ge(s_xkst[j], xk_stored(len(raw_order) * KT - 1 + j))
            sp.wait_ge(s_mm, mm_count("S", NB - 1, 3))
            sp.wait_ge(s_modst, 16 * 6)

            def load_xk(b):
                for k in range(KT):
                    n = b * KT + k
                    if n >= 2:
                        sp.wait_ge(s_xklo, n - 1)
                    sp.dma_start(xkr[:, n % 2], xk2_s[b, k]).then_inc(s_xkr[n % 2], 16)

            def load_bc2(b):
                if b:
                    sp.wait_ge(s_h5, TT * b)
                for i, m in enumerate((2, 4, 3)):
                    sp.dma_start(bc2[:, i], mod_s[m, b:b + 1, :].partition_broadcast(P)).then_inc(s_bc2, 16)

            def load_tile(t):
                if t >= NT:
                    return
                if t >= 2:
                    sp.wait_ge(s_x4, t - 1)
                for i, src in enumerate((x2_s, x_d)):
                    sp.dma_start(ld[:, t % 2, i], src[t]).then_inc(s_ld[t % 2], 16)

            def load_sr(b):
                for j in range(TT):
                    t = b * TT + j
                    if b:
                        sp.wait_ge(s_x4st[t % 2], 16 * (t // 2 - 1))
                        sp.wait_ge(s_hcb, t - TT + 1)
                    sp.dma_start(x4b[:, j], sr_s[b * TT + j]).then_inc(s_lds[j], 16)

            def store_tile(t):
                sp.wait_ge(s_x4, t + 1)
                sp.dma_start(x4_s[t], x4b[:, t % TT]).then_inc(s_x4st[t % 2], 16)
                load_tile(t + 2)
                sp.wait_ge(s_h5, t + 1)
                sp.dma_start(h5_s[t], h5b[:, t % 2]).then_inc(s_h5st[t % 2], 16)

            def store_h5T(t):
                sp.wait_ge(s_h5T, t + 1)
                j = t % TT
                sp.dma_start(h5T_s[t // TT, :, :, j * P:(j + 1) * P], h5T[:, t % 2]).then_inc(s_h5Tst[t % 2], 16)

            def load_h5r(b):
                for k in range(KT):
                    n = b * KT + k
                    if n == 0:
                        sp.wait_ge(s_kk, NB * MF)
                        sp.wait_ge(s_h5Tst[0], 32)
                        sp.wait_ge(s_h5Tst[1], 32)
                    if n >= 2:
                        sp.wait_ge(s_htlo, n - 1)
                    sp.dma_start(h5r[:, n % 2], h5T_s[b, :, k, :]).then_inc(s_h5r[n % 2], 16)

            load_xk(0)
            load_bc2(0)
            load_sr(0)
            load_tile(0)
            load_tile(1)
            for n in range(20, 26):
                load_half(n, cm_half(n))
            for b in range(NB):
                if b == NB - 1:
                    for n in range(26, 34):
                        load_half(n, ex_half(n))
                if b + 1 < NB:
                    load_xk(b + 1)
                if b == NB - 1:
                    load_h5r(0)
                for j in range(TT):
                    t = b * TT + j
                    store_tile(t)
                    if t >= 1:
                        store_h5T(t - 1)
                if b + 1 < NB:
                    load_bc2(b + 1)
                    load_sr(b + 1)
                if b == NB - 1:
                    store_h5T(NT - 1)

            for i in range(2):
                sp.wait_ge(s_x4st[i], 16 * NT // 2)
                sp.wait_ge(s_h5st[i], 16 * NT // 2)
                sp.wait_ge(s_h5Tst[i], 16 * NT // 2)
            sp.wait_ge(s_h5, NT)
            sp.wait_ge(s_rt, NT)

            def load_gb(b):
                if b:
                    sp.wait_ge(s_gsh, b * TT)
                sp.dma_start(gb_bc[:, :], mod_s[5, b:b + 1, :].partition_broadcast(P)).then_inc(s_gb, 16)

            def load_x4(t):
                if t >= 2:
                    sp.wait_ge(s_base, t - 1)
                sp.dma_start(x4l[:, t % 2], x4_s[t]).then_inc(s_x4l[t % 2], 16)

            def store_base(t):
                sp.wait_ge(s_base, t + 1)
                sp.dma_start(base_s[t], yb[:, t % 2]).then_inc(s_basest[t % 2], 16)

            def load_h5l(t):
                if t >= 4:
                    sp.wait_ge(s_scat[t % 4], 32 * (t // 4))
                sp.dma_start(h5l[:, t % 4], h5_s[t]).then_inc(s_h5l[t % 4], 16)

            load_h5r(1)
            for n in range(34, 40):
                load_half(n, ex_half(n))
            load_gb(0)
            load_x4(0)
            load_x4(1)
            for t in range(4):
                load_h5l(t)
            for b in range(NB):
                if b + 2 < NB:
                    load_h5r(b + 2)
                for j in range(TT):
                    t = b * TT + j
                    store_base(t)
                    if t + 2 < NT:
                        load_x4(t + 2)
                    if b >= 2:
                        for q in (2 * t - NT, 2 * t - NT + 1):
                            if q + 4 < NT:
                                load_h5l(q + 4)
                if b + 1 < NB:
                    load_gb(b + 1)
            for i in range(4):
                sp.wait_ge(s_scat[i], 32 * NT // 4)
            for i in range(2):
                sp.wait_ge(s_basest[i], 16 * NT // 2)
            sp.wait_ge(s_zero, 16 * (2 * NSX - FULL))
            sp.wait_ge(s_dn, NT)
            for b in range(NB):
                sp.dma_start(gb2[:, b], mod_s[5, b:b + 1, :].partition_broadcast(P)).then_inc(s_gb2, 16)

            def rows(a, q):
                return a.rearrange("(s p) h -> s p h", p=P)[bass.ds(q, 1)].rearrange("s p h -> (s p) h")

            def load_xs(q, par, wait=None):
                if wait is not None:
                    sp.wait_ge(s_tx, wait)
                sp.dma_start(xsb[:, par], rows(xs_s, q)).then_inc(s_xs[par], 16)

            def store_y(q, par, count):
                sp.wait_ge(s_y4, count)
                sp.dma_start(rows(ys_s, q), ysb[:, par]).then_inc(s_yst[par], 16)

            load_xs(0, 0)
            load_xs(1, 1)
            load_xs(2, 0, 1)
            store_y(0, 0, AHEAD + 1)
            pairs = sp.value_load(tend[0:1, NE:NE + 1], min_val=NE // 2, max_val=NS // 2)
            with sp.Fori(0, pairs) as i:
                load_xs(i * 2 + 3, 1, i * 2 + 2)
                store_y(i * 2 + 1, 1, i * 2 + 2 + AHEAD)
                load_xs(i * 2 + 4, 0, i * 2 + 3)
                store_y(i * 2 + 2, 0, i * 2 + 3 + AHEAD)
            sp.wait_ge(s_yst[0], pairs * 16 + 32)
            sp.sem_inc(s_end, 1)
            sp.wait_ge(s_yst[1], pairs * 16 + 16)
            sp.sem_inc(s_end, 1)
            def load_base(t):
                if t >= 4:
                    sp.wait_ge(s_o4, t - 3)
                sp.dma_start(bsb[:, t % 4], base_s[t]).then_inc(s_h5l[t % 4], 16)

            for t in range(NT):
                load_base(t)
                if t >= 2:
                    sp.wait_ge(s_o4, t - 1)
                    sp.dma_start(out_d[t - 2], g1b[:, (t - 2) % 4]).then_inc(s_out[(t - 2) % 4], 16)
            for t in (NT - 2, NT - 1):
                sp.wait_ge(s_o4, t + 1)
                sp.dma_start(out_d[t], g1b[:, t % 4]).then_inc(s_out[t % 4], 16)
            for i in range(4):
                sp.wait_ge(s_out[i], 16 * NT // 4)

        @block.tensor
        def _(pe):
            def modulation(i):
                pe.wait_ge(s_wmod[i], 16)
                for k in range(KT):
                    mm = pe.matmul(mm_ps[i % 4][0:NB, :], cT[:, k, :], wmod[:, i, k, :],
                                   start=k == 0, stop=k == KT - 1)
                mm.then_inc(s_modps, 1)

            def turn(kind, b):
                for j in range(TT):
                    n = hn_count(kind, b, j)
                    pe.wait_ge(s_hn, n)
                    if n > 2:
                        pe.wait_ge(s_hT, n - 2)
                    for k in range(KT):
                        mm = pe.transpose(tp_ps[(n - 1) % 2][:, k, :], hn[:, (n - 1) % 2, k * P:(k + 1) * P],
                                          ident[:, :])
                    mm.then_inc(s_tp, 1)

            def channels_out(s, b):
                m_ = mix[:, mix_slot(s, b)]
                if b == 0:
                    n = 2 * (w_load_order.index(s) + 1)
                    pe.wait_ge(s_whi, n)
                    pe.wait_ge(s_wlo, n)
                for m in range(KT):
                    bank_free(pe, s, b, m)
                    for k in range(KT):
                        if m == 0:
                            pe.wait_ge(s_mhi, split_count(s, b, k))
                            pe.wait_ge(s_mlo, split_count(s, b, k))
                        w = [w_of[s][:, i, k, m * P:(m + 1) * P] for i in range(2)]
                        mm = mm3(pe, mm_ps[m][:, :], w, [m_[:, i, k, :] for i in range(2)],
                                 k == 0, k == KT - 1)
                    mm.then_inc(s_mm, 1)

            def tokens_out(s, b):
                if b == 0:
                    n = 2 * (w_load_order.index(s) + 1)
                    pe.wait_ge(s_whi, n)
                    pe.wait_ge(s_wlo, n)
                m_ = rw if s == "O" else mix[:, mix_slot(s, b)]
                for j in range(TT):
                    bank_free(pe, s, b, j)
                    for k in range(KT):
                        if j == 0:
                            if s == "O":
                                pe.wait_ge(s_rwhi, b * KT + k + 1)
                                pe.wait_ge(s_rwlo, b * KT + k + 1)
                            else:
                                pe.wait_ge(s_mhi, split_count(s, b, k))
                                pe.wait_ge(s_mlo, split_count(s, b, k))
                        a = [m_[:, i, k, j * P:(j + 1) * P] for i in range(2)]
                        mm = mm3(pe, mm_ps[j][:, :], a, [w_of[s][:, i, k, :] for i in range(2)],
                                 k == 0, k == KT - 1)
                    mm.then_inc(s_mm, 1)

            pe.wait_ge(s_const, 2)
            pe.wait_ge(s_csil, 2)
            modulation(0)
            modulation(1)
            turn(1, 0)
            for i in range(2, 6):
                if i >= 4:
                    pe.wait_ge(s_modsb, i - 3)
                modulation(i)
            pe.wait_ge(s_modsb, 6)
            for b in range(NB):
                channels_out("K", b)
                channels_out("V", b)
                if b:
                    turn(2, b - 1)
                channels_out("R", b)
                if b:
                    tokens_out("S", b - 1)
                if b + 1 < NB:
                    turn(1, b + 1)
                tokens_out("O", b)
            turn(2, NB - 1)
            tokens_out("S", NB - 1)

            def key(g):
                b, m = divmod(g, MF)
                u = 2 * (m // KT)
                if m == 0:
                    if b == 0:
                        pe.wait_ge(s_sr, NT)
                        pe.wait_ge(s_hT, hT_count(2, NB - 1))
                        pe.wait_ge(s_x2, NT)
                        pe.wait_ge(s_sig, NT)
                if b == 0 and m % KT == 0:
                    pe.wait_ge(s_whi, 10 + 2 * (u + 1))
                    pe.wait_ge(s_wlo, 10 + 2 * (u + 1))
                if g >= 2:
                    pe.wait_ge(s_silo, g - 1)
                for k in range(KT):
                    if m == 0:
                        pe.wait_ge(s_xkhi, b * KT + k + 1)
                        pe.wait_ge(s_xklo, b * KT + k + 1)
                    w = [cm_unit(u)[:, i, k, (m % KT) * P:(m % KT + 1) * P] for i in range(2)]
                    mm = mm3(pe, kk_ps[g % 2][:, :], w, [xk[:, i, k, :] for i in range(2)], k == 0, k == KT - 1)
                mm.then_inc(s_kk, 1)

            def value(g):
                b, m = divmod(g, MF)
                u = 2 * (m // KT) + 1
                if b == 0 and m % KT == 0:
                    pe.wait_ge(s_whi, 10 + 2 * (u + 1))
                    pe.wait_ge(s_wlo, 10 + 2 * (u + 1))
                pe.wait_ge(s_sihi, g + 1)
                pe.wait_ge(s_silo, g + 1)
                for j in range(TT):
                    if m == 0 and b:
                        pe.wait_ge(s_kvr, (b - 1) * TT + j + 1)
                    a = [silu[:, g % NSILU, i, j * P:(j + 1) * P] for i in range(2)]
                    mm = mm3(pe, kv_ps[j][:, :], a, [cm_unit(u)[:, i, m % KT, :] for i in range(2)],
                             m == 0, m == MF - 1)
                mm.then_inc(s_kv, 1)

            def turn5(t):
                pe.wait_ge(s_h5, t + 1)
                if t:
                    pe.wait_ge(s_h5T, t)
                for k in range(KT):
                    mm = pe.transpose(t5_ps[:, k, :], h5b[:, t % 2, k * P:(k + 1) * P], ident[:, :])
                mm.then_inc(s_t5, 1)

            def router(t):
                pe.wait_ge(s_h5T, t + 1)
                for k in range(KT):
                    mm = pe.matmul(rt_ps[:, t, :], h5T[:, t % 2, k, :], wrt[:, k, :], start=k == 0, stop=k == KT - 1)
                mm.then_inc(s_rt, 1)

            for g in range(NB * MF + 2):
                if g < NB * MF:
                    key(g)
                if g >= 2:
                    value(g - 2)
                b, m = divmod(g, MF)
                if b and 4 <= m < 4 + TT:
                    turn5((b - 1) * TT + m - 4)
                if b and 5 <= m < 5 + TT:
                    router((b - 1) * TT + m - 5)
            def shared_up(b):
                for m in range(KT):
                    n = b * KT + m
                    if n >= 2:
                        pe.wait_ge(s_midlo, n - 1)
                    else:
                        pe.wait_ge(s_silo, NB * MF)
                    if n == 0:
                        pe.wait_ge(s_whi, 28)
                        pe.wait_ge(s_wlo, 28)
                    for k in range(KT):
                        if m == 0:
                            pe.wait_ge(s_hthi, b * KT + k + 1)
                            pe.wait_ge(s_htlo, b * KT + k + 1)
                        w = [ex_w[:, 0, i, k * H + m * P:k * H + (m + 1) * P] for i in range(2)]
                        mm = mm3(pe, up_ps[n % 2][:, :], w, [ht[:, i, k, :] for i in range(2)], k == 0, k == KT - 1)
                    mm.then_inc(s_up, 1)

            def shared_down(b):
                if b == 0:
                    pe.wait_ge(s_whi, 30)
                    pe.wait_ge(s_wlo, 30)
                for j in range(TT):
                    t = b * TT + j
                    if t >= 3:
                        pe.wait_ge(s_gsh, t - 2)
                    else:
                        pe.wait_ge(s_kvr, NT)
                    for k in range(KT):
                        if j == 0:
                            pe.wait_ge(s_midhi, b * KT + k + 1)
                            pe.wait_ge(s_midlo, b * KT + k + 1)
                        a = [mid[:, b % 2, i, k, j * P:(j + 1) * P] for i in range(2)]
                        w = [ex_w[:, 1, i, k * H:(k + 1) * H] for i in range(2)]
                        mm = mm3(pe, dn_ps[t % 3][:, :], a, w, k == 0, k == KT - 1)
                    mm.then_inc(s_dn, 1)

            def prefix_sums():
                pe.wait_ge(s_cho, 1)
                pe.wait_ge(s_con, 12)
                c = chosen[:, :, :].rearrange("p t e -> p (t e)")
                pe.matmul(pf_ps[:, 0].rearrange("p t e -> p (t e)"), upper[:, :], c, start=True, stop=True)
                pe.matmul(pf_ps[:, 1].rearrange("p t e -> p (t e)"), onesb[:, :].to_broadcast([P, P]), c, start=True, stop=True)\
                    .then_inc(s_pf, 1)

            shared_up(0)
            for j in range(TT):
                turn5(NT - TT + j)
                router(NT - TT + j)
            shared_up(1)
            shared_down(0)
            shared_up(2)
            prefix_sums()
            shared_down(1)
            shared_up(3)
            shared_down(2)
            shared_down(3)

            pe.wait_ge(s_pos, 1)
            pe.wait_ge(s_gsh, NT)

            def turn_x(q, par, xs_count, free_count):
                pe.wait_ge(s_xs[par], xs_count)
                if free_count is not None:
                    pe.wait_ge(s_txhi, free_count)
                    pe.wait_ge(s_txlo, free_count)
                for k in range(KT):
                    mm = pe.transpose(xs_ps[par][:, k, :], xsb[:, par, k * P:(k + 1) * P], ident[:, :])
                mm.then_inc(s_tx, 1)

            def up(q, par, count, free_count):
                e = pe.value_load(tab[0:1, 0, bass.ds(q, 1)], min_val=0, max_val=NE - 1)
                r = pe.value_load(tab[0:1, 1, bass.ds(q, 1)], min_val=0, max_val=RING - 1)
                pe.wait_ge(s_exr, e + 1)
                pe.wait_ge(s_txhi, count)
                pe.wait_ge(s_txlo, count)
                if free_count is not None:
                    pe.wait_ge(s_g4, free_count)
                for k in range(KT):
                    a = [xsT[:, par, i, k, :] for i in range(2)]
                    w = [ex_w[:, bass.ds(r, 1), i, k * (H // 2):(k + 1) * (H // 2)].rearrange("p a c -> p (a c)")
                         for i in range(2)]
                    mm = mm3(pe, up4_ps[par][:, 0:H // 2], a, w, k == 0, k == KT - 1)
                mm.then_inc(s_u4, 1)

            def turn_m(q, par, count, free_count):
                pe.wait_ge(s_g4, count)
                if free_count is not None:
                    pe.wait_ge(s_tmhi, free_count)
                    pe.wait_ge(s_tmlo, free_count)
                for k in range(2):
                    mm = pe.transpose(tm_ps[:, k, :], mb[:, par, k * P:(k + 1) * P], ident[:, :])
                mm.then_inc(s_tm, 1)

            def down(q, par, count, free_count):
                r = pe.value_load(tab[0:1, 1, bass.ds(q, 1)], min_val=0, max_val=RING - 1)
                pe.wait_ge(s_tmhi, count)
                pe.wait_ge(s_tmlo, count)
                pe.wait_ge(s_y4, free_count)
                for k in range(2):
                    a = [mbT[:, par, i, k, :] for i in range(2)]
                    w = [ex_w[:, bass.ds(r, 1), i, HALF + k * H:HALF + (k + 1) * H].rearrange("p a c -> p (a c)")
                         for i in range(2)]
                    mm = mm3(pe, dn4_ps[par][:, :], a, w, k == 0, k == 1)
                mm.then_inc(s_d4, 1)

            turn_x(0, 0, 16, None)
            up(0, 0, 1, None)
            turn_x(1, 1, 16, None)
            turn_m(0, 0, 1, None)
            pairs = pe.value_load(tend[0:1, NE:NE + 1], min_val=NE // 2, max_val=NS // 2)
            with pe.Fori(0, pairs) as i:
                up(i * 2 + 1, 1, i * 2 + 2, i * 2 + 1)
                turn_x(i * 2 + 2, 0, i * 16 + 32, i * 2 + 1)
                down(i * 2, 0, i * 2 + 1, i * 2 + 1)
                turn_m(i * 2 + 1, 1, i * 2 + 2, i * 2 + 1)
                up(i * 2 + 2, 0, i * 2 + 3, i * 2 + 2)
                turn_x(i * 2 + 3, 1, i * 16 + 32, i * 2 + 2)
                down(i * 2 + 1, 1, i * 2 + 2, i * 2 + 2)
                turn_m(i * 2 + 2, 0, i * 2 + 3, i * 2 + 2)
            down(pairs * 2, 0, pairs * 2 + 1, pairs * 2 + 1)

        @block.vector
        def _(dve):
            own = Count(s_dve)

            def done(ins):
                dve.wait_ge(s_dve, own.up(ins))

            dve.memset(hT[:, :, 0:1], 0.0).then_inc(s_const, 1)
            dve.wait_ge(s_csil, 1)
            dve.tensor_tensor(cT[:, :, :], cT[:, :, :], sgc[:, :, :], ALU.mult).then_inc(s_csil, 1)

            def variance(src, st, mv, t, kind, s_out):
                j = t % TT
                if t >= TT:
                    dve.wait_ge(s_out, t - TT + 1)
                    dve.wait_ge(s_hn, hn_count(kind, t // TT - 1, j))
                done(dve.bn_stats(st[:, j], src))
                done(dve.bn_aggr(mv[:, j], st[:, j]))
                dve.tensor_scalar(mv[:, j, 1:2], mv[:, j, 1:2], EPS, None, ALU.add).then_inc(s_out, 1)

            def first_norm_a(b, j):
                t = b * TT + j
                dve.wait_ge(s_x[j], 16 * (b + 1))
                variance(xb[:, j], st1, mv1, t, 1, s_st1)

            def first_norm_b(b, j):
                t = b * TT + j
                dve.wait_ge(s_rs1, t + 1)
                done(dve.tensor_scalar(xb[:, j], xb[:, j], mv1[:, j, 0:1], rs1[:, j:j + 1],
                                       ALU.subtract, ALU.mult))
                dve.wait_ge(s_bc, 32 * (b + 1))
                dve.tensor_tensor(xb[:, j], xb[:, j], ca_bc[:, :], ALU.mult).then_inc(s_hca, 1)

            def first_norm_c(b, j):
                t = b * TT + j
                dve.wait_ge(s_h0, t + 1)
                variance(xb[:, j], st2, mv2, t, 1, s_st2)

            def first_norm(b):
                for i in range(TT + 2):
                    if i < TT:
                        first_norm_a(b, i)
                    if 1 <= i <= TT:
                        first_norm_b(b, i - 1)
                    if i >= 2:
                        first_norm_c(b, i - 2)

            def hn_out(kind, b, src, mv, rs, s_r):
                for j in range(TT):
                    t = b * TT + j
                    n = hn_count(kind, b, j)
                    dve.wait_ge(s_r, t + 1)
                    if n > 2:
                        dve.wait_ge(s_tp, n - 2)
                    dve.tensor_scalar(hn[:, (n - 1) % 2], src[:, j], mv[:, j, 0:1], rs[:, j:j + 1],
                                      ALU.subtract, ALU.mult).then_inc(s_hn, 1)

            def differences(kind, b):
                dve.wait_ge(s_hT, hT_count(kind, b))
                for k in range(KT):
                    ins = dve.tensor_tensor(dT[:, k, :], hT[:, k, 1:T + 1], hT[:, k, 0:T], ALU.subtract)
                    ins.then_inc(s_dT, 1)
                dve.wait_ge(s_dT, turns.index((kind, b)) * KT + KT)

            def mixed(s, b):
                vec = {"K": V_MK, "V": V_MV, "R": V_MR, "X": V_CK, "S": V_CR}[s]
                for k in range(KT):
                    n = raw_count(s, b, k)
                    if n > 2:
                        i, kk = divmod(n - 3, KT)
                        s0, b0 = raw_order[i]
                        if s0 == "X":
                            dve.wait_ge(s_xkst[(n - 1) % 2], xk_stored(n - 2))
                        else:
                            dve.wait_ge(s_mhi, split_count(s0, b0, kk))
                            dve.wait_ge(s_mlo, split_count(s0, b0, kk))
                    dve.scalar_tensor_tensor(out=raw[:, (n - 1) % 2], in0=dT[:, k, :], scalar=vecs[:, vec, k:k + 1],
                                             in1=hT[:, k, 0:T], op0=ALU.mult, op1=ALU.add).then_inc(s_raw, 1)

            def k_out(b):
                for m in range(KT):
                    f = vecs[:, V_FIRST, m:m + 1]
                    dve.wait_ge(s_mm, mm_count("K", b, m))
                    if b:
                        dve.wait_ge(s_rwlo, (b - 1) * KT + m + 1)
                    done(dve.tensor_scalar(eT[:, m, :], mm_ps[m][:, :], f, PP0, ALU.add, ALU.max))
                    dve.scalar_tensor_tensor(out=eT[:, m, :], in0=mm_ps[m][:, :], scalar=f, in1=eT[:, m, :],
                                             op0=ALU.add, op1=ALU.subtract).then_inc(s_ke, 1)

            def v_out(b):
                for m in range(KT):
                    dve.wait_ge(s_e2, b * KT + m + 1)
                    dve.wait_ge(s_mm, mm_count("V", b, m))
                    done(dve.tensor_tensor(eT[:, m, :], mm_ps[m][:, :], eT[:, m, :], ALU.mult))
                    dve.tensor_tensor(eT[:, m, :], eT[:, m, :], rec[:, m % 2], ALU.mult).then_inc(s_va, 1)

            def r_out(b):
                for m in range(KT):
                    dve.wait_ge(s_sig, b * KT + m + 1)
                    dve.wait_ge(s_va, b * KT + m + 1)
                    dve.tensor_tensor(eT[:, m, :], eT[:, m, :], sig[:, m % 2], ALU.mult).then_inc(s_rw, 1)
                    dve.wait_ge(s_rwhi, b * KT + m + 1)
                    dve.tensor_tensor(rw[:, 1, m, :], eT[:, m, :], rw[:, 0, m, :].bitcast(F32),
                                      ALU.subtract).then_inc(s_rwlo, 1)

            def o_out(b):
                for j in range(TT):
                    t = b * TT + j
                    dve.wait_ge(s_mm, mm_count("O", b, j))
                    dve.wait_ge(s_h0r[t % 2], 16 * (t // 2 + 1))
                    if b:
                        dve.wait_ge(s_x2st[j], 16 * b)
                        dve.wait_ge(s_hn, hn_count(2, b - 1, j))
                    dve.tensor_tensor(x2b[:, j], mm_ps[j][:, :], h0r[:, t % 2], ALU.add).then_inc(s_x2, 1)
                    dve.wait_ge(s_x2, t + 1)
                    variance(x2b[:, j], st3, mv3, t, 2, s_st3)

            for i in range(6):
                dve.wait_ge(s_modps, i + 1)
                if i == 5:
                    dve.wait_ge(s_modsb, 5)
                src = mm_ps[i % 4][0:NB, :]
                if i in (0, 3):
                    ins = dve.tensor_copy(modr[:, i], src)
                elif i in (1, 4):
                    ins = dve.tensor_scalar(modr[:, i], src, 1.0, None, ALU.add)
                else:
                    done(dve.tensor_scalar(modt[:, 0], src, 0.0, 2.0, ALU.is_ge, ALU.mult))
                    done(dve.tensor_scalar(modt[:, 1], src, -1.0, 0.25, ALU.mult, ALU.max))
                    done(dve.tensor_tensor(modt[:, 1], src, modt[:, 1], ALU.max))
                    done(dve.tensor_scalar(modt[:, 0], modt[:, 0], -1.0, None, ALU.add))
                    ins = dve.tensor_tensor(modr[:, i], modt[:, 0], modt[:, 1], ALU.mult)
                ins.then_inc(s_modsb, 1)
                if i == 1:
                    first_norm(0)
                    hn_out(1, 0, xb, mv2, rs2, s_rs2)
            differences(1, 0)
            mixed("K", 0)
            mixed("V", 0)
            for b in range(NB):
                k_out(b)
                if b + 1 < NB:
                    first_norm(b + 1)
                v_out(b)
                mixed("R", b)
                if b:
                    hn_out(2, b - 1, x2b, mv3, rs3, s_rs3)
                    differences(2, b - 1)
                    mixed("X", b - 1)
                    mixed("S", b - 1)
                r_out(b)
                if b + 1 < NB:
                    hn_out(1, b + 1, xb, mv2, rs2, s_rs2)
                    differences(1, b + 1)
                    mixed("K", b + 1)
                    mixed("V", b + 1)
                o_out(b)
            hn_out(2, NB - 1, x2b, mv3, rs3, s_rs3)
            differences(2, NB - 1)
            mixed("X", NB - 1)
            mixed("S", NB - 1)

            def silu_lo(g):
                dve.wait_ge(s_sihi, g + 1)
                dve.tensor_tensor(silu[:, g % NSILU, 1, :], kk_ps[g % 2][:, :], silu[:, g % NSILU, 0, :].bitcast(F32),
                                  ALU.subtract).then_inc(s_silo, 1)

            def post_a(t):
                dve.wait_ge(s_kv, (t // TT + 1) * MF)
                dve.wait_ge(s_lds[t % TT], 16 * (t // TT + 1))
                if t >= TT:
                    dve.wait_ge(s_gx3, t - TT + 1)
                dve.tensor_tensor(x4b[:, t % TT], kv_ps[t % TT][:, :], x4b[:, t % TT], ALU.mult).then_inc(s_kvr, 1)

            def post_b(t):
                dve.wait_ge(s_x3, t + 1)
                dve.wait_ge(s_bc2, 48 * (t // TT + 1))
                dve.tensor_tensor(x4b[:, t % TT], x4b[:, t % TT], bc2[:, 0], ALU.mult).then_inc(s_gx3, 1)

            def post_c(t):
                dve.wait_ge(s_x4, t + 1)
                if t >= 2:
                    dve.wait_ge(s_rs5, t - 1)
                done(dve.bn_stats(st5[:, t % 2], x4b[:, t % TT]))
                done(dve.bn_aggr(mv5[:, t % 2], st5[:, t % 2]))
                dve.tensor_scalar(mv5[:, t % 2, 1:2], mv5[:, t % 2, 1:2], EPS, None, ALU.add).then_inc(s_st5, 1)

            def post_d(t):
                dve.wait_ge(s_rs5, t + 1)
                if t >= 2:
                    dve.wait_ge(s_h5st[t % 2], 16 * (t // 2))
                    dve.wait_ge(s_t5, t - 1)
                done(dve.tensor_scalar(h5b[:, t % 2], x4b[:, t % TT], mv5[:, t % 2, 0:1], rs5[:, t % 2:t % 2 + 1],
                                       ALU.subtract, ALU.mult))
                dve.tensor_tensor(h5b[:, t % 2], h5b[:, t % 2], bc2[:, 1], ALU.mult).then_inc(s_hcb, 1)

            for g in range(NB * MF):
                silu_lo(g)
                b, m = divmod(g, MF)
                if b and m == 1:
                    for j in range(TT):
                        post_a((b - 1) * TT + j)
                if b and 1 <= m < 1 + TT:
                    post_b((b - 1) * TT + m - 1)
                if b and 2 <= m < 2 + TT:
                    t = (b - 1) * TT + m - 2
                    post_c(t)
                    post_d(t)
            def mid_lo(n):
                b, m = divmod(n, KT)
                dve.wait_ge(s_midhi, n + 1)
                dve.tensor_tensor(mid[:, b % 2, 1, m, :], up_ps[n % 2][:, :], mid[:, b % 2, 0, m, :].bitcast(F32),
                                  ALU.subtract).then_inc(s_midlo, 1)

            def gb_shared(t):
                dve.wait_ge(s_dn, t + 1)
                dve.wait_ge(s_gb, 16 * (t // TT + 1))
                if t >= 2:
                    dve.wait_ge(s_basest[t % 2], 16 * (t // 2))
                dve.tensor_tensor(yb[:, t % 2], dn_ps[t % 3][:, :], gb_bc[:, :], ALU.mult).then_inc(s_gsh, 1)

            def per_token(v):
                return v.rearrange("p (t a) -> p t a", a=1).to_broadcast([P, NT, NE])

            def per_expert(v):
                return v.rearrange("p (a e) -> p a e", a=1).to_broadcast([P, NT, NE])

            def choose(c):
                g = gates[:, c, :]
                done(dve.tensor_reduce(g, pr[:, :, :], AX.X, ALU.max))
                done(dve.tensor_tensor(tmp[:, :, :], pr[:, :, :], per_token(g), ALU.is_equal))
                done(dve.tensor_tensor(tmp[:, :, :], tmp[:, :, :], per_expert(rev[:, :]), ALU.mult))
                done(dve.tensor_reduce(red[:, :], tmp[:, :, :], AX.X, ALU.max))
                done(dve.tensor_tensor(oh[:, c], per_expert(rev[:, :]), per_token(red[:, :]), ALU.is_equal))

            def route():
                dve.wait_ge(s_con, 12)
                dve.wait_ge(s_rt, NT)
                done(dve.tensor_copy(lg[:, :, :], rt_ps[:, :, :]))
                done(dve.tensor_reduce(red[:, :], lg[:, :, :], AX.X, ALU.max))
                dve.tensor_tensor(lg[:, :, :], lg[:, :, :], per_token(red[:, :]), ALU.subtract).then_inc(s_sub, 1)
                dve.wait_ge(s_exp, 1)
                done(dve.tensor_reduce(red[:, :], pr[:, :, :], AX.X, ALU.add))
                done(dve.reciprocal(red2[:, :], red[:, :]))
                done(dve.tensor_tensor(pr[:, :, :], pr[:, :, :], per_token(red2[:, :]), ALU.mult))
                choose(0)
                done(dve.scalar_tensor_tensor(out=pr[:, :, :], in0=oh[:, 0], scalar=-2.0, in1=pr[:, :, :],
                                              op0=ALU.mult, op1=ALU.add))
                choose(1)
                dve.tensor_tensor(chosen[:, :, :], oh[:, 0], oh[:, 1], ALU.add).then_inc(s_cho, 1)

            def place():
                dve.wait_ge(s_pf, 1)
                done(dve.memset(off[:, 0, :], 0.0))
                for t in range(NT):
                    done(dve.tensor_tensor(off[:, t + 1, :], off[:, t, :], pf_ps[:, 1, t, :], ALU.add))
                count = off[:, NT, :]
                done(dve.tensor_tensor(tmp[:, 0:NE, :], count.rearrange("p (e a) -> p e a", a=1)
                                       .to_broadcast([P, NE, NE]),
                                       thr[:, :].rearrange("p (a k) -> p a k", a=1).to_broadcast([P, NE, NE]),
                                       ALU.is_gt))
                done(dve.tensor_reduce(ntile[:, :], tmp[:, 0:NE, :], AX.X, ALU.add))
                done(dve.tensor_tensor_scan(tends[:, :], ones16[:, :].to_broadcast([P, NE]), ntile[:, :], 0.0, ALU.mult, ALU.add))
                done(dve.tensor_tensor(ntile[:, :], tends[:, :], ntile[:, :], ALU.subtract))
                done(dve.tensor_scalar(ntile[:, :], ntile[:, :], float(P), None, ALU.mult))
                done(dve.tensor_tensor(off[:, 0:NT, :], off[:, 0:NT, :], per_expert(ntile[:, :]), ALU.add))
                done(dve.tensor_tensor(off[:, 0:NT, :], off[:, 0:NT, :], pf_ps[:, 0], ALU.add))
                for c in range(2):
                    done(dve.tensor_tensor(tmp[:, :, :], off[:, 0:NT, :], oh[:, c], ALU.mult))
                    done(dve.tensor_reduce(red[:, :], tmp[:, :, :], AX.X, ALU.add))
                    done(dve.tensor_copy(pos[:, c, :], red[:, :]))
                done(dve.tensor_tensor(cmp[:, :, :],
                                       tends[0:1, :].rearrange("p (a e) -> p a e", a=1).to_broadcast([1, NSX, NE]),
                                       sidx[:, :].rearrange("p (s a) -> p s a", a=1).to_broadcast([1, NSX, NE]),
                                       ALU.is_le))
                done(dve.tensor_reduce(tabf[:, 0], cmp[:, :, :], AX.X, ALU.add))
                done(dve.tensor_scalar(tabf[:, 0], tabf[:, 0], float(NE - 1), None, ALU.min))
                done(dve.tensor_copy(tab[:, 0], tabf[:, 0]))
                done(dve.tensor_scalar(tabf[:, 1], tabf[:, 0], float(BASE), None, ALU.add))
                for r in range(RING, NE - 1 + BASE + 1, RING):
                    done(dve.tensor_scalar(tabf[:, 2], tabf[:, 0], float(r - BASE), float(-RING), ALU.is_ge, ALU.mult))
                    done(dve.tensor_tensor(tabf[:, 1], tabf[:, 1], tabf[:, 2], ALU.add))
                done(dve.tensor_copy(tab[:, 1], tabf[:, 1]))
                done(dve.tensor_copy(tend[:, 0:NE], tends[0:1, :]))
                done(dve.tensor_reduce(tabf[:, 3, 0:1], thr2(), AX.X, ALU.add))
                dve.tensor_copy(tend[:, NE:NE + 1], tabf[:, 3, 0:1]).then_inc(s_pos, 1)

            def thr2():
                done(dve.tensor_scalar(tabf[:, 2, :], sidx[:, :], 2.0, 1.0, ALU.mult, ALU.add))
                done(dve.tensor_scalar(tabf[:, 2, :], tabf[:, 2, :], tends[0:1, NE - 1:NE], None, ALU.is_lt))
                return tabf[:, 2, :]

            for j in range(TT):
                post_a(NT - TT + j)
            for i in range(TT + 1):
                t = NT - TT + i
                if i < TT:
                    post_b(t)
                if i:
                    post_c(t - 1)
                    post_d(t - 1)
                if i < TT:
                    mid_lo(i)
            for m in range(KT):
                mid_lo(KT + m)
            route()
            for t in range(TT):
                gb_shared(t)
            for m in range(KT):
                mid_lo(2 * KT + m)
            place()
            for t in range(TT, 2 * TT):
                gb_shared(t)
            for m in range(KT):
                mid_lo(3 * KT + m)
            for t in range(2 * TT, NT):
                gb_shared(t)

            def turned_lo(par, count):
                dve.wait_ge(s_txhi, count)
                dve.tensor_tensor(xsT[:, par, 1], xs_ps[par][:, :, :], xsT[:, par, 0].bitcast(F32), ALU.subtract)\
                    .then_inc(s_txlo, 1)

            def turned_mid_lo(par, count):
                dve.wait_ge(s_tmhi, count)
                dve.tensor_tensor(mbT[:, par, 1], tm_ps[:, 0:2, :], mbT[:, par, 0].bitcast(F32), ALU.subtract)\
                    .then_inc(s_tmlo, 1)

            def y_out(par, count, stored):
                dve.wait_ge(s_d4, count)
                if stored is not None:
                    dve.wait_ge(s_yst[par], stored)
                dve.tensor_copy(ysb[:, par], dn4_ps[par][:, :]).then_inc(s_y4, 1)

            dve.sem_inc(s_y4, AHEAD)
            dve.sem_inc(s_yst[1], 16)
            dve.sem_inc(s_yst[0], 16)
            turned_lo(0, 1)
            turned_lo(1, 2)
            turned_mid_lo(0, 1)
            pairs = dve.value_load(tend[0:1, NE:NE + 1], min_val=NE // 2, max_val=NS // 2)
            with dve.Fori(0, pairs) as i:
                turned_lo(0, i * 2 + 3)
                y_out(0, i * 2 + 1, i * 16 + 16)
                turned_mid_lo(1, i * 2 + 2)
                turned_lo(1, i * 2 + 4)
                y_out(1, i * 2 + 2, i * 16 + 16)
                turned_mid_lo(0, i * 2 + 3)
            y_out(0, pairs * 2 + 1, pairs * 16 + 16)

            for t in range(NT):
                b = t // TT
                dve.wait_ge(s_o1, t + 1)
                done(dve.scalar_tensor_tensor(out=g1b[:, t % 4], in0=g2b[:, t % 4], scalar=gates[:, 1, t:t + 1],
                                              in1=g1b[:, t % 4], op0=ALU.mult, op1=ALU.add))
                dve.wait_ge(s_gb2, 16 * NB)
                done(dve.tensor_tensor(g1b[:, t % 4], g1b[:, t % 4], gb2[:, b], ALU.mult))
                dve.wait_ge(s_h5l[t % 4], 16 * (NT // 4 + t // 4 + 1))
                dve.tensor_tensor(g1b[:, t % 4], g1b[:, t % 4], bsb[:, t % 4], ALU.add).then_inc(s_o4, 1)

        @block.scalar
        def _(act):
            act.wait_ge(s_small, 48)
            act.activation(sgc[:, :, :], cT[:, :, :], ACT.Sigmoid).then_inc(s_csil, 1)

            def weight_hi(n):
                act.wait_ge(s_stage[n % 2], 16 * (n // 2 + 1))
                if n == 4:
                    act.wait_ge(s_modps, 6)
                if n < 10:
                    w = w_of[w_load_order[n // 2]]
                elif n >= 26:
                    u = (n - 26) // 2
                    w = ex_w[:, u].rearrange("p i (k c) -> p i k c", c=H)
                    act.wait_ge(*ex_free()[u])
                else:
                    w = cm_unit((n - 10) // 2)
                    act.wait_ge(s_mm, cm_free()[(n - 10) // 2])
                k0 = (n % 2) * KT // 2
                act.activation(w[:, 0, k0:k0 + KT // 2, :], stage[:, n % 2].rearrange("p (k c) -> p k c", c=H),
                               ACT.Copy).then_inc(s_whi, 1)

            def to_hT(kind, b):
                g, o = (V_G1, V_B1) if kind == 1 else (V_G2, V_B2)
                i = turns.index((kind, b))
                if i:
                    k0, b0 = turns[i - 1]
                    last = ("R", b0) if k0 == 1 else ("S", b0)
                    act.wait_ge(s_raw, raw_count(*last, KT - 1))
                for j in range(TT):
                    n = hn_count(kind, b, j)
                    act.wait_ge(s_tp, n)
                    for k in range(KT):
                        ins = act.activation(hT[:, k, 1 + j * P:1 + (j + 1) * P], tp_ps[(n - 1) % 2][:, k, :],
                                             ACT.Identity, scale=vecs[:, g, k:k + 1], bias=vecs[:, o, k:k + 1])
                    ins.then_inc(s_hT, 1)

            def mixed_hi(s, b):
                i = split_order.index((s, b))
                for k in range(KT):
                    act.wait_ge(s_raw, raw_count(s, b, k))
                    if i >= 2 and k == 0:
                        act.wait_ge(s_mm, mm_count(*split_order[i - 2], 3))
                    act.activation(mix[:, i % 2, 0, k, :], raw[:, (raw_count(s, b, k) - 1) % 2], ACT.Copy)\
                        .then_inc(s_mhi, 1)

            def exps(b):
                for m in range(KT):
                    n = b * KT + m
                    act.wait_ge(s_ke, n + 1)
                    if n >= 2:
                        act.wait_ge(s_va, n - 1)
                    act.activation(rec[:, m % 2], eT[:, m, :], ACT.Exp, scale=-1.0).then_inc(s_rec, 1)
                    act.wait_ge(s_rec, n + 1)
                    act.activation(eT[:, m, :], eT[:, m, :], ACT.Exp).then_inc(s_e2, 1)

            def sigmoids(b):
                for m in range(KT):
                    n = b * KT + m
                    act.wait_ge(s_mm, mm_count("R", b, m))
                    if n >= 2:
                        act.wait_ge(s_rw, n - 1)
                    act.activation(sig[:, m % 2], mm_ps[m][:, :], ACT.Sigmoid).then_inc(s_sig, 1)
                    if m:
                        rw_hi(b, m - 1)
                rw_hi(b, KT - 1)

            def rw_hi(b, m):
                act.wait_ge(s_rw, b * KT + m + 1)
                if m == 0:
                    if b:
                        act.wait_ge(s_mm, mm_count("O", b - 1, 3))
                    else:
                        act.wait_ge(s_modst, 16 * 6)
                act.activation(rw[:, 0, m, :], eT[:, m, :], ACT.Copy).then_inc(s_rwhi, 1)

            def sr_out(b):
                for j in range(TT):
                    t = b * TT + j
                    act.wait_ge(s_mm, mm_count("S", b, j))
                    if t >= 2:
                        act.wait_ge(s_srst[t % 2], 16 * (t // 2))
                    act.activation(srb[:, t % 2], mm_ps[j][:, :], ACT.Sigmoid).then_inc(s_sr, 1)

            for n in range(4):
                weight_hi(n)
            to_hT(1, 0)
            mixed_hi("K", 0)
            mixed_hi("V", 0)
            for n in range(4, 10):
                weight_hi(n)
            for b in range(NB):
                exps(b)
                mixed_hi("R", b)
                if b:
                    to_hT(2, b - 1)
                    mixed_hi("S", b - 1)
                sigmoids(b)
                if b:
                    sr_out(b - 1)
                if b + 1 < NB:
                    to_hT(1, b + 1)
                    mixed_hi("K", b + 1)
                    mixed_hi("V", b + 1)
                else:
                    for n in range(10, 16):
                        weight_hi(n)
            to_hT(2, NB - 1)
            mixed_hi("S", NB - 1)
            sr_out(NB - 1)

            def xk_hi(b):
                for k in range(KT):
                    n = b * KT + k
                    act.wait_ge(s_xkr[n % 2], 16 * (n // 2 + 1))
                    if b:
                        act.wait_ge(s_kk, b * MF)
                    act.activation(xk[:, 0, k, :], xkr[:, n % 2], ACT.Copy).then_inc(s_xkhi, 1)

            def silu_hi(g):
                act.wait_ge(s_kk, g + 1)
                act.activation(kk_ps[g % 2][:, :], kk_ps[g % 2][:, :], ACT.Silu).then_inc(s_silu, 1)
                act.wait_ge(s_silu, g + 1)
                if g >= NSILU:
                    act.wait_ge(s_kv, g - NSILU + 1)
                act.activation(silu[:, g % NSILU, 0, :], kk_ps[g % 2][:, :], ACT.Copy).then_inc(s_sihi, 1)

            def to_h5T(t):
                act.wait_ge(s_t5, t + 1)
                if t >= 2:
                    act.wait_ge(s_h5Tst[t % 2], 16 * (t // 2))
                    act.wait_ge(s_rt, t - 1)
                act.activation(h5T[:, t % 2], t5_ps[:, :, :], ACT.Copy).then_inc(s_h5T, 1)

            for n in range(16, 18):
                weight_hi(n)
            xk_hi(0)
            for g in range(NB * MF):
                b, m = divmod(g, MF)
                silu_hi(g)
                if b == 0 and g < 4:
                    weight_hi(18 + 2 * g)
                    weight_hi(19 + 2 * g)
                if b and 4 <= m < 4 + TT:
                    to_h5T((b - 1) * TT + m - 4)
                if m == MF - 1 and b + 1 < NB:
                    xk_hi(b + 1)
                if b == NB - 1 and m >= 6 and m % 2 == 0 and m < 14:
                    weight_hi(20 + m)
                    weight_hi(21 + m)

            def ht_hi(b):
                for k in range(KT):
                    n = b * KT + k
                    act.wait_ge(s_h5r[n % 2], 16 * (n // 2 + 1))
                    if b:
                        act.wait_ge(s_up, b * KT)
                    act.activation(ht[:, 0, k, :], h5r[:, n % 2], ACT.Copy).then_inc(s_hthi, 1)

            def gelu(b):
                for m in range(KT):
                    n = b * KT + m
                    act.wait_ge(s_up, n + 1)
                    act.activation(up_ps[n % 2][:, :], up_ps[n % 2][:, :], ACT.Gelu).then_inc(s_gelu, 1)
                    act.wait_ge(s_gelu, n + 1)
                    if b == 0 and m == 0:
                        act.wait_ge(s_kv, NB * MF)
                    if b >= 2:
                        act.wait_ge(s_dn, (b - 1) * TT)
                    act.activation(mid[:, b % 2, 0, m, :], up_ps[n % 2][:, :], ACT.Copy).then_inc(s_midhi, 1)

            ht_hi(0)
            gelu(0)
            for j in range(TT):
                to_h5T(NT - TT + j)
            ht_hi(1)
            for n in range(34, 40):
                weight_hi(n)
            gelu(1)
            act.wait_ge(s_sub, 1)
            act.activation(pr[:, :, :], lg[:, :, :], ACT.Exp).then_inc(s_exp, 1)
            ht_hi(2)
            gelu(2)
            ht_hi(3)
            gelu(3)

            def turned_hi(par, count):
                act.wait_ge(s_tx, count)
                act.activation(xsT[:, par, 0], xs_ps[par][:, :, :], ACT.Copy).then_inc(s_txhi, 1)

            def gelu4(par, count):
                act.wait_ge(s_u4, count)
                act.activation(mb[:, par], up4_ps[par][:, 0:H // 2], ACT.Gelu).then_inc(s_g4, 1)

            def turned_mid_hi(par, count):
                act.wait_ge(s_tm, count)
                act.activation(mbT[:, par, 0], tm_ps[:, 0:2, :], ACT.Copy).then_inc(s_tmhi, 1)

            turned_hi(0, 1)
            gelu4(0, 1)
            turned_hi(1, 2)
            turned_mid_hi(0, 1)
            pairs = act.value_load(tend[0:1, NE:NE + 1], min_val=NE // 2, max_val=NS // 2)
            with act.Fori(0, pairs) as i:
                gelu4(1, i * 2 + 2)
                turned_hi(0, i * 2 + 3)
                turned_mid_hi(1, i * 2 + 2)
                gelu4(0, i * 2 + 3)
                turned_hi(1, i * 2 + 4)
                turned_mid_hi(0, i * 2 + 3)

            for t in range(NT):
                act.wait_ge(s_scat[t % 4], 32 * (NT // 4 + t // 4 + 1))
                act.activation(g1b[:, t % 4], g1b[:, t % 4], ACT.Copy, scale=gates[:, 0, t:t + 1]).then_inc(s_o1, 1)

        @block.gpsimd
        def _(pool):
            pool.memset(ident[:, :], 0.0).then_inc(s_id, 1)
            pool.wait_ge(s_id, 1)
            pool.affine_select(out=ident[:, :], in_=ident[:, :], compare_op=ALU.not_equal, fill=1.0, base=0,
                               pattern=[[-1, P]], channel_multiplier=1).then_inc(s_const, 1)
            pool.memset(zero[:, :], 0.0).then_inc(s_con, 1)
            pool.memset(onesb[:, :], 1.0).then_inc(s_con, 1)
            pool.memset(upper[:, :], 1.0).then_inc(s_con, 1)
            pool.memset(ones16[:, :], 1.0).then_inc(s_con, 1)
            pool.iota(iot[:, 0:NE], [[128, NE]], base=0, channel_multiplier=0).then_inc(s_con, 1)
            pool.wait_ge(s_con, 5)
            pool.tensor_copy(thr[:, :], iot[:, 0:NE]).then_inc(s_con, 1)
            pool.affine_select(out=upper[:, :], in_=upper[:, :], compare_op=ALU.is_gt, fill=0.0, base=0,
                               pattern=[[1, P]], channel_multiplier=-1).then_inc(s_con, 1)
            pool.wait_ge(s_con, 7)
            pool.memset(thr[:, 0:1], -1.0).then_inc(s_con, 1)
            pool.iota(iot[:, 0:NE], [[-1, NE]], base=NE, channel_multiplier=0).then_inc(s_con, 1)
            pool.wait_ge(s_con, 9)
            pool.tensor_copy(rev[:, :], iot[:, 0:NE]).then_inc(s_con, 1)
            pool.wait_ge(s_con, 10)
            pool.iota(iot[:, :], [[1, NSX]], base=0, channel_multiplier=0).then_inc(s_con, 1)
            pool.wait_ge(s_con, 11)
            pool.tensor_copy(sidx[:, :], iot[0:1, :]).then_inc(s_con, 1)
            pool.memset(neghalf[:, :], -0.5).then_inc(s_id, 1)
            pool.wait_ge(s_id, 2)

            def weight_lo(n):
                if n < 10:
                    w = w_of[w_load_order[n // 2]]
                elif n < 26:
                    w = cm_unit((n - 10) // 2)
                else:
                    w = ex_w[:, (n - 26) // 2].rearrange("p i (k c) -> p i k c", c=H)
                k0 = (n % 2) * KT // 2
                pool.wait_ge(s_whi, n + 1)
                pool.tensor_tensor(w[:, 1, k0:k0 + KT // 2, :], stage[:, n % 2].rearrange("p (k c) -> p k c", c=H),
                                   w[:, 0, k0:k0 + KT // 2, :].bitcast(F32), ALU.subtract).then_inc(s_wlo, 1)

            def rsqrt(rs, mv, b, j, s_in, s_out):
                pool.wait_ge(s_in, b * TT + j + 1)
                pool.tensor_tensor(rs[:, j:j + 1], mv[:, j, 1:2], neghalf[:, :], ALU.pow).then_inc(s_out, 1)

            def first_norm(b):
                for i in range(TT + 1):
                    if i < TT:
                        rsqrt(rs1, mv1, b, i, s_st1, s_rs1)
                    if i >= 1:
                        j = i - 1
                        pool.wait_ge(s_hca, b * TT + j + 1)
                        pool.tensor_tensor(xb[:, j], xb[:, j], sa_bc[:, :], ALU.add).then_inc(s_h0, 1)
                    if i >= 2:
                        rsqrt(rs2, mv2, b, i - 2, s_st2, s_rs2)
                rsqrt(rs2, mv2, b, TT - 1, s_st2, s_rs2)

            def mixed_lo(s, b):
                i = split_order.index((s, b))
                for k in range(KT):
                    pool.wait_ge(s_mhi, split_count(s, b, k))
                    pool.tensor_tensor(mix[:, i % 2, 1, k, :], raw[:, (raw_count(s, b, k) - 1) % 2],
                                       mix[:, i % 2, 0, k, :].bitcast(F32), ALU.subtract).then_inc(s_mlo, 1)

            weight_lo(0)
            weight_lo(1)
            first_norm(0)
            weight_lo(2)
            weight_lo(3)
            mixed_lo("K", 0)
            mixed_lo("V", 0)
            for n in range(4, 10):
                weight_lo(n)
            for b in range(NB):
                if b + 1 < NB:
                    first_norm(b + 1)
                mixed_lo("R", b)
                if b:
                    mixed_lo("S", b - 1)
                if b + 1 < NB:
                    mixed_lo("K", b + 1)
                    mixed_lo("V", b + 1)
                for j in range(TT):
                    rsqrt(rs3, mv3, b, j, s_st3, s_rs3)
            for n in range(10, 16):
                weight_lo(n)
            mixed_lo("S", NB - 1)

            def xk_lo(b):
                for k in range(KT):
                    n = b * KT + k
                    pool.wait_ge(s_xkhi, n + 1)
                    pool.tensor_tensor(xk[:, 1, k, :], xkr[:, n % 2], xk[:, 0, k, :].bitcast(F32), ALU.subtract)\
                        .then_inc(s_xklo, 1)

            def post(t):
                pool.wait_ge(s_kvr, t + 1)
                pool.wait_ge(s_ld[t % 2], 32 * (t // 2 + 1))
                pool.tensor_tensor(x4b[:, t % TT], x4b[:, t % TT], ld[:, t % 2, 0], ALU.add).then_inc(s_x3, 1)
                pool.wait_ge(s_gx3, t + 1)
                pool.tensor_tensor(x4b[:, t % TT], x4b[:, t % TT], ld[:, t % 2, 1], ALU.add).then_inc(s_x4, 1)

            def post_norm(t):
                pool.wait_ge(s_st5, t + 1)
                if t >= 2:
                    pool.wait_ge(s_hcb, t - 1)
                pool.tensor_tensor(rs5[:, t % 2:t % 2 + 1], mv5[:, t % 2, 1:2], neghalf[:, :], ALU.pow)\
                    .then_inc(s_rs5, 1)
                pool.wait_ge(s_hcb, t + 1)
                pool.tensor_tensor(h5b[:, t % 2], h5b[:, t % 2], bc2[:, 2], ALU.add).then_inc(s_h5, 1)

            def posts(b):
                for i in range(TT + 1):
                    if i < TT:
                        post(b * TT + i)
                    if i:
                        post_norm(b * TT + i - 1)

            for n in range(16, 18):
                weight_lo(n)
            xk_lo(0)
            for n in range(18, 26):
                weight_lo(n)
            for b in range(NB):
                if b:
                    xk_lo(b)
                    posts(b - 1)
            for n in range(26, 34):
                weight_lo(n)

            def ht_lo(b):
                for k in range(KT):
                    n = b * KT + k
                    pool.wait_ge(s_hthi, n + 1)
                    pool.tensor_tensor(ht[:, 1, k, :], h5r[:, n % 2], ht[:, 0, k, :].bitcast(F32), ALU.subtract)\
                        .then_inc(s_htlo, 1)

            def base(t):
                pool.wait_ge(s_gsh, t + 1)
                pool.wait_ge(s_x4l[t % 2], 16 * (t // 2 + 1))
                pool.tensor_tensor(yb[:, t % 2], yb[:, t % 2], x4l[:, t % 2], ALU.add).then_inc(s_base, 1)

            def scatter(t):
                pool.wait_ge(s_h5l[t % 4], 16 * (t // 4 + 1))
                for c in range(2):
                    pool.indirect_dma_start(xs_s, bass.IndirectOffsetOnAxis(ap=pos[:, c, t:t + 1], axis=0),
                                            h5l[:, t % 4], None).then_inc(s_scat[t % 4], 16)

            ht_lo(0)
            posts(NB - 1)
            ht_lo(1)
            for n in range(34, 40):
                weight_lo(n)
            ht_lo(2)
            for t in range(TT):
                base(t)
            ht_lo(3)
            for t in range(TT, 2 * TT):
                base(t)
            pool.wait_ge(s_pos, 1)
            pool.wait_ge(s_zero, 16 * NSX)
            for t in range(2 * TT, NT):
                base(t)
                scatter(2 * t - NT)
                scatter(2 * t - NT + 1)
            pool.wait_ge(s_wlo, 40)
            pool.sem_inc(s_exr, PRE)

            def expert_load(n):
                if n >= 2:
                    pool.wait_ge(s_exd, 2 * (n - 1))
                e = PRE + n // 2
                pool.dma_start(stage[:, n % 2], wex_d[2 + e, :, (n % 2) * HALF:(n % 2 + 1) * HALF])\
                    .then_inc(s_exs[n % 2], 16)

            def expert_split(n):
                e = PRE + n // 2
                pool.wait_ge(s_exs[n % 2], 16 * (n // 2 + 1))
                if n % 2 == 0:
                    if e < RING:
                        pool.wait_ge(s_dn, NT)
                    else:
                        end = pool.value_load(tend[0:1, e - RING:e - RING + 1], min_val=1, max_val=NS)
                        pool.wait_ge(s_d4, end)
                half = slice((n % 2) * HALF, (n % 2 + 1) * HALF)
                hi, lo = (ex_w[:, ring_slot(e), i, half] for i in range(2))
                pool.tensor_tensor(hi, stage[:, n % 2], zero[:, 0:1].to_broadcast([P, HALF]), ALU.add).then_inc(s_exd, 1)
                pool.wait_ge(s_exd, 2 * n + 1)
                pool.tensor_tensor(lo, stage[:, n % 2], hi.bitcast(F32), ALU.subtract).then_inc(s_exd, 1)
                if n % 2:
                    pool.wait_ge(s_exd, 2 * n + 2)
                    pool.sem_inc(s_exr, 1)

            halves = 2 * (NE - PRE)
            expert_load(0)
            expert_load(1)
            for n in range(halves):
                expert_split(n)
                if n + 2 < halves:
                    expert_load(n + 2)

            pool.wait_ge(s_end, 2)
            for t in range(NT):
                if t >= 4:
                    pool.wait_ge(s_out[t % 4], 16 * (t // 4))
                for c, buf in ((0, g1b), (1, g2b)):
                    pool.indirect_dma_start(buf[:, t % 4], None, ys_s,
                                            bass.IndirectOffsetOnAxis(ap=pos[:, c, t:t + 1], axis=0))\
                        .then_inc(s_scat[t % 4], 16)


def kernel(**inputs):
    import numpy as np
    import concourse.bacc as bacc
    from concourse import mybir as mb
    from concourse.bass_utils import run_bass_kernel_spmd as run

    def tiled(w):
        k, n = w.shape
        return np.ascontiguousarray(w.reshape(k // 128, 128, n).transpose(1, 0, 2).reshape(128, -1))

    g = {k.removeprefix("L0_"): np.asarray(v) for k, v in inputs.items()}
    x = g["attn_x"].reshape(16, 128, 512)
    c = np.ascontiguousarray(g["c"].T.reshape(4, 128, 4).transpose(1, 0, 2))
    wmod = np.stack([tiled(g["wmod"][:, i * 512:(i + 1) * 512]).reshape(128, 4, 512) for i in range(6)])
    names = ["tm_mk", "tm_mv", "tm_mr", "cm_mk", "cm_mr", "ln1_g", "ln1_b", "ln2_g", "ln2_b", "tm_first"]
    vecs = np.ascontiguousarray(np.stack([g["attn_" + n].reshape(4, 128).T for n in names], axis=1))
    wtm = np.stack([tiled(g["attn_" + n].T) for n in ("Wk", "Wv", "Wr", "Wo", "Wcr")])
    wkey = g["attn_Wkey"].T
    wval = g["attn_Wval"].T
    wcm = np.stack([tiled(w) for j in range(4) for w in (wkey[:, j * 512:(j + 1) * 512], wval[j * 512:(j + 1) * 512])])
    up = [g["ffn_Wsh_up"].transpose(1, 0, 2).reshape(512, 512)]
    down = [g["ffn_Wsh_down"].reshape(512, 512)]
    wex = np.stack([tiled(up[0]), tiled(down[0])] +
                   [np.concatenate([tiled(g["ffn_Wrt_up"][e]), tiled(g["ffn_Wrt_down"][e])], axis=1) for e in range(16)])
    ins = {"x": x, "c": c, "wmod": wmod, "vecs": vecs, "wtm": wtm, "wcm": wcm,
           "wrt": tiled(g["ffn_W_router"]).reshape(128, 4, 16), "wex": wex}
    nc = bacc.Bacc("TRN2", target_bir_lowering=False, num_devices=1)
    arrays, args = {}, []
    for name, a in ins.items():
        a = np.ascontiguousarray(a)
        arrays[f"in_{name}"] = a
        args.append(nc.dram_tensor(f"in_{name}", a.shape, mb.dt.from_np(a.dtype), kind="ExternalInput").ap())
    out = nc.dram_tensor("out_0", (16, 128, 512), mb.dt.float32, kind="ExternalOutput").ap()
    adaln_block(nc, *args, out)
    r = run(nc, [arrays], core_ids=[0])
    return r.results[0]["out_0"].reshape(4, 512, 512)
```

```python
from contextlib import ExitStack

import concourse.bass as bass
from concourse import mybir

F32 = mybir.dt.float32
F32R = mybir.dt.float32r
BF16 = mybir.dt.bfloat16
I32 = mybir.dt.int32
ALU = mybir.AluOpType
ACT = mybir.ActivationFunctionType
AX = mybir.AxisListType

P = 128
H = 512
KT = H // P
NB = 4
T = 512
TT = T // P
NT = NB * TT
F = 4 * H
MF = F // P
EPS = 1e-5
UNIT = KT * H
HALF = UNIT // 2
NE = 16
NS = NB * T * 2 // P + NE
FULL = NB * T * 2 // P
NSX = NS + 4
RING = 7
BASE = 2
PRE = RING - BASE
AHEAD = 2
NH5 = 6
NG = 5
NSILU = 4
UNIT_SLOT = [0, 1, 2, 3, 7, 4, 5, 6]
PP0 = -1e38

V_MK, V_MV, V_MR, V_CK, V_CR, V_G1, V_B1, V_G2, V_B2, V_FIRST = range(10)


class Count:

    def __init__(self, sem, step=1):
        self.sem, self.step, self.n = sem, step, 0

    def up(self, ins):
        self.n += 1
        ins.then_inc(self.sem, self.step)
        return self.n


def adaln_block(nc, x_d, c_d, wmod_d, vecs_d, wtm_d, wcm_d, wrt_d, wex_d, out_d):
    top = ExitStack()
    with top:
        def sem(name):
            return top.enter_context(nc.semaphore(name))

        def sbuf(stack, name, shape, dt=F32):
            return stack.enter_context(nc.sbuf_tensor(name, shape, dt))

        def psum(stack, name, shape, dt=F32):
            return stack.enter_context(nc.psum_tensor(name, shape, dt))

        mod_s = nc.dram_tensor("mod_s", (6, NB, H), F32).ap()
        h0_s = nc.dram_tensor("h0_s", (NT, P, H), F32).ap()
        x2_s = nc.dram_tensor("x2_s", (NT, P, H), F32).ap()
        x4_s = nc.dram_tensor("x4_s", (NT, P, H), F32).ap()
        h5_s = nc.dram_tensor("h5_s", (NT, P, H), F32).ap()
        h5T_s = nc.dram_tensor("h5T_s", (NB, P, KT, T), F32).ap()
        base_s = nc.dram_tensor("base_s", (NT, P, H), F32).ap()
        xs_s = nc.dram_tensor("xs_s", (NSX * P, H), F32).ap()
        ys_s = nc.dram_tensor("ys_s", (NSX * P, H), F32).ap()
        sr_s = nc.dram_tensor("sr_s", (NT, P, H), F32).ap()
        xk2_s = nc.dram_tensor("xk2_s", (NB, KT, P, T), F32).ap()

        ident = sbuf(top, "ident", [P, P])
        vecs = sbuf(top, "vecs", [P, 10, KT])
        neghalf = sbuf(top, "neghalf", [P, 1])
        wrt = sbuf(top, "wrt", [P, KT, NE])
        gates = sbuf(top, "gates", [P, 2, NT])
        pos = sbuf(top, "pos", [P, 2, NT], I32)
        tab = sbuf(top, "tab", [1, 1, NSX], I32)
        tend = sbuf(top, "tend", [1, NE + 1], I32)
        zero = sbuf(top, "zero", [P, P])
        rev = sbuf(top, "rev", [P, NE])
        thr = sbuf(top, "thr", [P, NE])
        upper = sbuf(top, "upper", [P, P], BF16)
        onesb = sbuf(top, "onesb", [P, 1], BF16)
        ones16 = sbuf(top, "ones16", [P, 1])
        sidx = sbuf(top, "sidx", [1, NSX])
        iot = sbuf(top, "iot", [P, NSX], I32)
        stage = sbuf(top, "stage", [P, 2, HALF])

        ph1 = ExitStack()
        wkv_w = sbuf(ph1, "wkv_w", [P, 2, 2, KT, H], F32R)
        overlay = ExitStack()
        wmod = sbuf(overlay, "wmod", [P, 6, KT, H])
        overlay.close()
        wro_w = sbuf(ph1, "wro_w", [P, 3, 2, KT, H], F32R)
        mix = sbuf(ph1, "mix", [P, 2, 2, KT, T], F32R)
        overlay = ExitStack()
        modr = sbuf(overlay, "modr", [NB, 6, H])
        modt = sbuf(overlay, "modt", [NB, 2, H])
        overlay.close()
        rw = sbuf(ph1, "rw", [P, 2, KT, T], F32R)
        eT = sbuf(ph1, "eT", [P, KT, T])
        hT = sbuf(ph1, "hT", [P, KT, T + 1])
        dT = sbuf(ph1, "dT", [P, KT, T])
        rec = sbuf(ph1, "rec", [P, 2, T])
        sig = sbuf(ph1, "sig", [P, 2, T])
        raw = sbuf(ph1, "raw", [P, 2, T])
        xb = sbuf(ph1, "xb", [P, TT, H])
        hn = sbuf(ph1, "hn", [P, 2, H])
        h0r = sbuf(ph1, "h0r", [P, 2, H])
        x2b = sbuf(ph1, "x2b", [P, TT, H])
        ca_bc = sbuf(ph1, "ca_bc", [P, H])
        sa_bc = sbuf(ph1, "sa_bc", [P, H])
        st1 = sbuf(ph1, "st1", [P, TT, 6])
        mv1 = sbuf(ph1, "mv1", [P, TT, 2])
        rs1 = sbuf(ph1, "rs1", [P, TT])
        st2 = sbuf(ph1, "st2", [P, TT, 6])
        mv2 = sbuf(ph1, "mv2", [P, TT, 2])
        rs2 = sbuf(ph1, "rs2", [P, TT])
        st3 = sbuf(ph1, "st3", [P, TT, 6])
        mv3 = sbuf(ph1, "mv3", [P, TT, 2])
        rs3 = sbuf(ph1, "rs3", [P, TT])
        cT = sbuf(ph1, "cT", [P, KT, NB])
        sgc = sbuf(ph1, "sgc", [P, KT, NB])
        srb = sbuf(ph1, "srb", [P, 2, H])
        ps1 = ExitStack()
        mm_ps = [psum(ps1, f"mm_ps{i}", [P, 512]) for i in range(4)]
        tp_ps = [psum(ps1, f"tp_ps{i}", [P, KT, P]) for i in range(2)]
        ph1.close()
        ps1.close()

        ph2 = ExitStack()
        cm_w = sbuf(ph2, "cm_w", [P, 8, 2, KT, H], F32R)
        xkr = sbuf(ph2, "xkr", [P, 2, T])
        xk = sbuf(ph2, "xk", [P, 2, KT, T], F32R)
        silu = sbuf(ph2, "silu", [P, NSILU, 2, T], F32R)
        ld = sbuf(ph2, "ld", [P, 2, 2, H])
        bc2 = sbuf(ph2, "bc2", [P, 3, H])
        x4b = sbuf(ph2, "x4b", [P, TT, H])
        h5b = sbuf(ph2, "h5b", [P, 2, H])
        h5T = sbuf(ph2, "h5T", [P, 2, KT, P])
        st5 = sbuf(ph2, "st5", [P, 2, 6])
        mv5 = sbuf(ph2, "mv5", [P, 2, 2])
        rs5 = sbuf(ph2, "rs5", [P, 2])
        ps2 = ExitStack()
        kk_ps = [psum(ps2, f"kk_ps{i}", [P, 512]) for i in range(2)]
        kv_ps = [psum(ps2, f"kv_ps{i}", [P, 512]) for i in range(4)]
        t5_ps = psum(ps2, "t5_ps", [P, KT, P])
        rt_ps = psum(ps2, "rt_ps", [P, NT, NE])
        ph2.close()
        ps2.close()

        ph3 = ExitStack()
        ex_w = sbuf(ph3, "ex_w", [P, RING, 2, UNIT], F32R)
        ht = sbuf(ph3, "ht", [P, 2, KT, T], F32R)
        h5r = sbuf(ph3, "h5r", [P, 2, T])
        mid = sbuf(ph3, "mid", [P, 2, 2, KT, T], F32R)
        yb = sbuf(ph3, "yb", [P, 2, H])
        x4l = sbuf(ph3, "x4l", [P, 2, H])
        gb_bc = sbuf(ph3, "gb_bc", [P, H])
        h5l = sbuf(ph3, "h5l", [P, NH5, H])
        lg = sbuf(ph3, "lg", [P, NT, NE])
        pr = sbuf(ph3, "pr", [P, NT, NE])
        oh = sbuf(ph3, "oh", [P, 2, NT, NE])
        tmp = sbuf(ph3, "tmp", [P, NT, NE])
        red = sbuf(ph3, "red", [P, NT])
        red2 = sbuf(ph3, "red2", [P, NT])
        chosen = sbuf(ph3, "chosen", [P, NT, NE], BF16)
        off = sbuf(ph3, "off", [P, NT + 1, NE])
        ntile = sbuf(ph3, "ntile", [P, NE])
        tends = sbuf(ph3, "tends", [P, NE])
        cmp = sbuf(ph3, "cmp", [1, NSX, NE])
        tabf = sbuf(ph3, "tabf", [1, 4, NSX])
        ps3 = ExitStack()
        up_ps = [psum(ps3, f"up_ps{i}", [P, 512]) for i in range(2)]
        dn_ps = [psum(ps3, f"dn_ps{i}", [P, 512]) for i in range(3)]
        pf_ps = psum(ps3, "pf_ps", [P, 2, NT, NE])
        ph3.close()
        ps3.close()

        ph4 = ExitStack()
        sbuf(ph4, "ex_w4", [P, RING, 2, UNIT], F32R)
        bsb = sbuf(ph4, "bsb", [P, NT, H])
        gb2 = sbuf(ph4, "gb2", [P, NB, H])
        xsb = sbuf(ph4, "xsb", [P, 2, H])
        xsT = sbuf(ph4, "xsT", [P, 2, 2, KT, P], F32R)
        mb = sbuf(ph4, "mb", [P, 2, H // 2])
        mbT = sbuf(ph4, "mbT", [P, 2, 2, 2, P], F32R)
        ysb = sbuf(ph4, "ysb", [P, 2, H])
        g1b = sbuf(ph4, "g1b", [P, NG, H])
        g2b = sbuf(ph4, "g2b", [P, NG, H])
        ps4 = ExitStack()
        xs_ps = [psum(ps4, f"xs_ps{i}", [P, KT, P]) for i in range(2)]
        up4_ps = [psum(ps4, f"up4_ps{i}", [P, 512]) for i in range(2)]
        tm_ps = psum(ps4, "tm_ps", [P, KT, P])
        dn4_ps = [psum(ps4, f"dn4_ps{i}", [P, 512]) for i in range(2)]
        ph4.close()
        ps4.close()

        s_const = sem("s_const")
        s_small = sem("s_small")
        s_wmod = [sem(f"s_wmod{i}") for i in range(6)]
        s_csil = sem("s_csil")
        s_modps = sem("s_modps")
        s_modsb = sem("s_modsb")
        s_modst = sem("s_modst")
        s_stage = [sem("s_stage0"), sem("s_stage1")]
        s_whi = sem("s_whi")
        s_wlo = sem("s_wlo")
        s_x = [sem(f"s_xt{i}") for i in range(TT)]
        s_bc = sem("s_bc")
        s_st1 = sem("s_st1")
        s_rs1 = sem("s_rs1")
        s_hca = sem("s_hca")
        s_h0 = sem("s_h0")
        s_h0st = [sem(f"s_h0st{i}") for i in range(TT)]
        s_st2 = sem("s_st2")
        s_rs2 = sem("s_rs2")
        s_hn = sem("s_hn")
        s_tp = sem("s_tp")
        s_hT = sem("s_hT")
        s_dT = sem("s_dT")
        s_raw = sem("s_raw")
        s_mhi = sem("s_mhi")
        s_mlo = sem("s_mlo")
        s_mm = sem("s_mm")
        s_kw = sem("s_kw")
        s_ke = sem("s_ke")
        s_e2 = sem("s_e2")
        s_rec = sem("s_rec")
        s_vm = sem("s_vm")
        s_va = sem("s_va")
        s_sig = sem("s_sig")
        s_rw = sem("s_rw")
        s_rwhi = sem("s_rwhi")
        s_rwlo = sem("s_rwlo")
        s_sr = sem("s_sr")
        s_srst = [sem("s_srst0"), sem("s_srst1")]
        s_h0r = [sem("s_h0r0"), sem("s_h0r1")]
        s_x2 = sem("s_x2")
        s_x2st = [sem(f"s_x2st{i}") for i in range(TT)]
        s_st3 = sem("s_st3")
        s_rs3 = sem("s_rs3")
        s_xkst = [sem("s_xkst0"), sem("s_xkst1")]
        s_dve = sem("s_dve")
        s_con = sem("s_con")
        s_zero = sem("s_zero")
        s_h5r = [sem("s_h5r0"), sem("s_h5r1")]
        s_hthi = sem("s_hthi")
        s_htlo = sem("s_htlo")
        s_up = sem("s_up")
        s_gelu = sem("s_gelu")
        s_midhi = sem("s_midhi")
        s_midlo = sem("s_midlo")
        s_dn = sem("s_dn")
        s_gsh = sem("s_gsh")
        s_base = sem("s_base")
        s_gb = sem("s_gb")
        s_x4l = [sem("s_x4l0"), sem("s_x4l1")]
        s_basest = [sem("s_basest0"), sem("s_basest1")]
        s_sub = sem("s_sub")
        s_exp = sem("s_exp")
        s_cho = sem("s_cho")
        s_pf = sem("s_pf")
        s_pos = sem("s_pos")
        s_h5l = [sem(f"s_h5l{i}") for i in range(NH5)]
        s_scat = [sem(f"s_scat{i}") for i in range(NH5)]
        s_exr = sem("s_exr")
        s_exs = [sem("s_exs0"), sem("s_exs1")]
        s_exd = sem("s_exd")
        s_xs = [sem("s_xs0"), sem("s_xs1")]
        s_tx = sem("s_tx")
        s_txhi = sem("s_txhi")
        s_txlo = sem("s_txlo")
        s_u4 = sem("s_u4")
        s_g4 = sem("s_g4")
        s_tm = sem("s_tm")
        s_tmhi = sem("s_tmhi")
        s_tmlo = sem("s_tmlo")
        s_d4 = sem("s_d4")
        s_y4 = sem("s_y4")
        s_yst = [sem("s_yst0"), sem("s_yst1")]
        s_end = sem("s_end")
        s_bsl = sem("s_bsl")
        s_o1 = sem("s_o1")
        s_o4 = sem("s_o4")
        s_out = s_h0st + s_x2st[:NG - TT]
        s_xkr = [sem("s_xkr0"), sem("s_xkr1")]
        s_xkhi = sem("s_xkhi")
        s_xklo = sem("s_xklo")
        s_kk = sem("s_kk")
        s_silu = sem("s_silu")
        s_sihi = sem("s_sihi")
        s_silo = sem("s_silo")
        s_kv = sem("s_kv")
        s_kvr = sem("s_kvr")
        s_ld = [sem("s_ld0"), sem("s_ld1")]
        s_lds = [sem(f"s_lds{i}") for i in range(TT)]
        s_bc2 = sem("s_bc2")
        s_x3 = sem("s_x3")
        s_gx3 = sem("s_gx3")
        s_x4 = sem("s_x4")
        s_st5 = sem("s_st5")
        s_rs5 = sem("s_rs5")
        s_hcb = sem("s_hcb")
        s_h5 = sem("s_h5")
        s_x4st = [sem("s_x4st0"), sem("s_x4st1")]
        s_h5st = [sem("s_h5st0"), sem("s_h5st1")]
        s_t5 = sem("s_t5")
        s_h5T = sem("s_h5T")
        s_h5Tst = [sem("s_h5Tst0"), sem("s_h5Tst1")]
        s_rt = sem("s_rt")
        s_id = sem("s_id")

        order1 = []
        for b in range(NB):
            order1 += [("K", b), ("V", b), ("R", b)]
            if b:
                order1.append(("S", b - 1))
            order1.append(("O", b))
        order1.append(("S", NB - 1))
        turns = [(1, 0)]
        for b in range(NB):
            if b:
                turns.append((2, b - 1))
            if b + 1 < NB:
                turns.append((1, b + 1))
        turns.append((2, NB - 1))
        used_by = {"K": s_kw, "V": s_vm, "R": s_sig, "S": s_sr, "O": s_x2}
        block = top.enter_context(nc.Block())

        def mm3(pe, out, lhs, rhs, first, last):
            pe.matmul(out, lhs[0], rhs[0], start=first, stop=False)
            pe.matmul(out, lhs[0], rhs[1], start=False, stop=False)
            return pe.matmul(out, lhs[1], rhs[0], start=False, stop=last)

        w_of = {"K": wkv_w[:, 0], "V": wkv_w[:, 1], "R": wro_w[:, 0], "O": wro_w[:, 1], "S": wro_w[:, 2]}
        w_load_order = ["K", "V", "R", "O", "S"]

        raw_order = [("K", 0), ("V", 0)]
        for b in range(NB):
            raw_order.append(("R", b))
            if b:
                raw_order += [("S", b - 1), ("X", b - 1)]
            if b + 1 < NB:
                raw_order += [("K", b + 1), ("V", b + 1)]
        raw_order += [("S", NB - 1), ("X", NB - 1)]
        split_order = [r for r in raw_order if r[0] != "X"]

        def xk_stored(n):
            return 16 * sum(1 for i in range(n) if i % 2 == (n - 1) % 2 and raw_order[i // KT][0] == "X")

        def cm_half(n):
            n -= 10
            return wcm_d[n // 2, :, (n % 2) * HALF:(n % 2 + 1) * HALF]

        def ex_half(n):
            n -= 26
            return wex_d[n // 2, :, (n % 2) * HALF:(n % 2 + 1) * HALF]

        def h5l_uses(i):
            return len(range(i, NT, NH5))

        def ring_slot(e):
            return (BASE + e) % RING

        def ex_free():
            last = (NB - 1) * MF
            return [(s_kk, last + 4), (s_kv, last + 4), (s_kk, last + 8), (s_kv, last + 8),
                    (s_kv, last + 12), (s_kk, last + 16), (s_kv, last + 16)]

        def cm_unit(u):
            return cm_w[:, UNIT_SLOT[u]]

        def cm_free():
            return [mm_count("K", NB - 1, 3), mm_count("V", NB - 1, 3), mm_count("R", NB - 1, 3),
                    mm_count("O", NB - 1, 3), mm_count("O", NB - 1, 3)] + 3 * [mm_count("S", NB - 1, 3)]

        def raw_count(s, b, k):
            return raw_order.index((s, b)) * KT + k + 1

        def split_count(s, b, k):
            return split_order.index((s, b)) * KT + k + 1

        def hn_count(kind, b, j):
            return turns.index((kind, b)) * TT + j + 1

        def hT_count(kind, b):
            return (turns.index((kind, b)) + 1) * TT

        def stage_index(s, b):
            return order1.index((s, b))

        def mm_count(s, b, j):
            return order1.index((s, b)) * 4 + j + 1

        def mix_slot(s, b):
            return split_order.index((s, b)) % 2

        def bank_free(eng, s, b, j):
            i = stage_index(s, b)
            if i == 0:
                return
            s0, b0 = order1[i - 1]
            eng.wait_ge(used_by[s0], b0 * 4 + j + 1)

        @block.sync
        def _(sp):
            sp.dma_start(cT[:, :, :], c_d).then_inc(s_small, 16)
            sp.dma_start(vecs[:, :, :], vecs_d).then_inc(s_small, 16)
            sp.dma_start(wrt[:, :, :], wrt_d).then_inc(s_small, 16)
            for i in (0, 1):
                sp.dma_start(wmod[:, i], wmod_d[i]).then_inc(s_wmod[i], 16)

            nx = [0]

            def load_x(b, tiles=range(TT)):
                for j in tiles:
                    t = b * TT + j
                    if b:
                        sp.wait_ge(s_h0st[j], 16 * b)
                        sp.wait_ge(s_hn, hn_count(1, b - 1, j))
                    sp.dma_start(xb[:, j], x_d[t]).then_inc(s_x[j], 16)

            def load_bc(b):
                if b == 0:
                    sp.wait_ge(s_modst, 32)
                else:
                    sp.wait_ge(s_h0, TT * b)
                sp.dma_start(ca_bc[:, :], mod_s[1, b:b + 1, :].partition_broadcast(P)).then_inc(s_bc, 16)
                sp.dma_start(sa_bc[:, :], mod_s[0, b:b + 1, :].partition_broadcast(P)).then_inc(s_bc, 16)

            def load_half(n, src):
                if n >= 2:
                    sp.wait_ge(s_whi, n - 1)
                    sp.wait_ge(s_wlo, n - 1)
                sp.dma_start(stage[:, n % 2], src).then_inc(s_stage[n % 2], 16)

            def clear_slots(i):
                n = -(-NSX // NB)
                sp.wait_ge(s_con, 1)
                for q in range(i * n, min(NSX, (i + 1) * n)):
                    for rows_s in (xs_s, ys_s):
                        if rows_s is xs_s or q >= FULL:
                            sp.dma_start(rows_s[q * P:(q + 1) * P, :].rearrange("p (k c) -> p k c", k=KT),
                                         zero[:, :].rearrange("p (k c) -> p k c", k=1).to_broadcast([P, KT, P]))\
                                .then_inc(s_zero, 16)

            def load_tm(n):
                load_half(n, wtm_d[n // 2, :, (n % 2) * HALF:(n % 2 + 1) * HALF])

            load_x(0)
            load_tm(0)
            load_tm(1)
            sp.wait_ge(s_modsb, 2)
            for i in (0, 1):
                sp.dma_start(mod_s[i], modr[:, i]).then_inc(s_modst, 16)
            load_bc(0)
            for i in range(2, 6):
                sp.dma_start(wmod[:, i], wmod_d[i]).then_inc(s_wmod[i], 16)
            load_tm(2)
            load_tm(3)

            def store_h0(b, tiles=range(TT)):
                for j in tiles:
                    t = b * TT + j
                    sp.wait_ge(s_h0, t + 1)
                    sp.dma_start(h0_s[t], xb[:, j]).then_inc(s_h0st[j], 16)

            def load_h0(b, tiles):
                for j in tiles:
                    t = b * TT + j
                    sp.wait_ge(s_h0st[j], 16 * (b + 1))
                    if t >= 2:
                        sp.wait_ge(s_x2, t - 1)
                    sp.dma_start(h0r[:, t % 2], h0_s[t]).then_inc(s_h0r[t % 2], 16)

            def store_x2(b, tiles):
                for j in tiles:
                    t = b * TT + j
                    sp.wait_ge(s_x2, t + 1)
                    sp.dma_start(x2_s[t], x2b[:, j]).then_inc(s_x2st[j], 16)

            def store_xk(b):
                for k in range(KT):
                    n = b * KT + k
                    sp.wait_ge(s_raw, raw_count("X", b, k))
                    sp.dma_start(xk2_s[b, k], raw[:, (raw_count("X", b, k) - 1) % 2]).then_inc(
                        s_xkst[(raw_count("X", b, k) - 1) % 2], 16)

            def load_xk(b, tiles=range(KT)):
                for k in tiles:
                    n = b * KT + k
                    if n >= 2:
                        sp.wait_ge(s_xklo, n - 1)
                    sp.dma_start(xkr[:, n % 2], xk2_s[b, k]).then_inc(s_xkr[n % 2], 16)

            def store_sr(b, tiles=range(TT)):
                for j in tiles:
                    t = b * TT + j
                    sp.wait_ge(s_sr, t + 1)
                    sp.dma_start(sr_s[t], srb[:, t % 2]).then_inc(s_srst[t % 2], 16)

            store_h0(0)
            load_bc(1)
            load_x(1)
            sp.wait_ge(s_modsb, 6)
            for i in range(2, 6):
                sp.dma_start(mod_s[i], modr[:, i]).then_inc(s_modst, 16)
            sp.wait_ge(s_modps, 6)
            for n in (4, 5, 6, 7):
                load_tm(n)
            for b in range(NB):
                if b + 1 < NB:
                    store_h0(b + 1, [0, 1, 2])
                load_h0(b, [0, 1])
                if b:
                    store_xk(b - 1)
                if b + 1 < NB:
                    store_h0(b + 1, [3])
                if b == 0:
                    load_tm(8)
                    load_tm(9)
                if b:
                    store_sr(b - 1, [0, 1])
                if b + 2 < NB:
                    load_bc(b + 2)
                    load_x(b + 2)
                if b:
                    store_sr(b - 1, [2, 3])
                if b == NB - 1:
                    load_half(10, cm_half(10))
                    load_half(11, cm_half(11))
                store_x2(b, [0])
                load_h0(b, [2])
                store_x2(b, [1])
                load_h0(b, [3])
                store_x2(b, [2, 3])
            load_half(12, cm_half(12))
            load_half(13, cm_half(13))
            for n in range(2):
                sp.wait_ge(s_xkst[n], xk_stored((len(raw_order) - 1) * KT - 1 + n))
            sp.wait_ge(s_rwlo, NB * KT)
            load_xk(0, [0, 1])
            store_xk(NB - 1)
            load_xk(0, [2, 3])
            store_sr(NB - 1, [0, 1])
            load_half(14, cm_half(14))
            load_half(15, cm_half(15))
            store_sr(NB - 1, [2, 3])
            for n in range(16, 26):
                load_half(n, cm_half(n))
            for j in range(TT):
                sp.wait_ge(s_x2st[j], 16 * NB)
            for j in range(2):
                sp.wait_ge(s_srst[j], 16 * NT // 2)
            for j in range(2):
                sp.wait_ge(s_xkst[j], xk_stored(len(raw_order) * KT - 1 + j))
            sp.wait_ge(s_mm, mm_count("S", NB - 1, 3))
            sp.wait_ge(s_modst, 16 * 6)

            def load_bc2(b):
                if b:
                    sp.wait_ge(s_h5, TT * b)
                for i, m in enumerate((2, 4, 3)):
                    sp.dma_start(bc2[:, i], mod_s[m, b:b + 1, :].partition_broadcast(P)).then_inc(s_bc2, 16)

            def load_tile(t):
                if t >= NT:
                    return
                if t >= 2:
                    sp.wait_ge(s_x4, t - 1)
                for i, src in enumerate((x2_s, x_d)):
                    sp.dma_start(ld[:, t % 2, i], src[t]).then_inc(s_ld[t % 2], 16)

            def load_sr(b):
                for j in range(TT):
                    t = b * TT + j
                    if b:
                        sp.wait_ge(s_x4st[t % 2], 16 * (t // 2 - 1))
                        sp.wait_ge(s_hcb, t - TT + 1)
                    sp.dma_start(x4b[:, j], sr_s[b * TT + j]).then_inc(s_lds[j], 16)

            def store_tile(t):
                sp.wait_ge(s_x4, t + 1)
                sp.dma_start(x4_s[t], x4b[:, t % TT]).then_inc(s_x4st[t % 2], 16)
                load_tile(t + 2)
                sp.wait_ge(s_h5, t + 1)
                sp.dma_start(h5_s[t], h5b[:, t % 2]).then_inc(s_h5st[t % 2], 16)

            def store_h5T(t):
                sp.wait_ge(s_h5T, t + 1)
                j = t % TT
                sp.dma_start(h5T_s[t // TT, :, :, j * P:(j + 1) * P], h5T[:, t % 2]).then_inc(s_h5Tst[t % 2], 16)

            def load_h5r(n):
                b, k = divmod(n, KT)
                if n == 0:
                    sp.wait_ge(s_xklo, NB * KT)
                if k == 0:
                    for i in range(2):
                        sp.wait_ge(s_h5Tst[i], 32 * (b + 1))
                if n >= 2:
                    sp.wait_ge(s_htlo, n - 1)
                sp.dma_start(h5r[:, n % 2], h5T_s[b, :, k, :]).then_inc(s_h5r[n % 2], 16)

            load_bc2(0)
            load_sr(0)
            load_tile(0)
            load_tile(1)
            for b in range(NB):
                if b == NB - 1:
                    for n in range(26, 36):
                        if n == 34:
                            load_h5r(0)
                            load_h5r(1)
                        load_half(n, ex_half(n))
                    load_h5r(2)
                    load_h5r(3)
                if b + 1 < NB:
                    load_xk(b + 1)
                clear_slots(b)
                if b == NB - 1:
                    load_h5r(KT)
                for j in range(TT):
                    t = b * TT + j
                    store_tile(t)
                    if b == NB - 1:
                        for n in {0: (5,), 1: (6, 7)}.get(j, ()):
                            load_h5r(n)
                    if t >= 1:
                        store_h5T(t - 1)
                if b + 1 < NB:
                    load_bc2(b + 1)
                    load_sr(b + 1)

            for i in range(2):
                sp.wait_ge(s_x4st[i], 16 * NT // 2)
            sp.wait_ge(s_h5, NT)

            def load_gb(b):
                if b:
                    sp.wait_ge(s_gsh, b * TT)
                sp.dma_start(gb_bc[:, :], mod_s[5, b:b + 1, :].partition_broadcast(P)).then_inc(s_gb, 16)

            def load_x4(t):
                if t >= 2:
                    sp.wait_ge(s_base, t - 1)
                sp.dma_start(x4l[:, t % 2], x4_s[t]).then_inc(s_x4l[t % 2], 16)

            def store_base(t):
                sp.wait_ge(s_base, t + 1)
                sp.dma_start(base_s[t], yb[:, t % 2]).then_inc(s_basest[t % 2], 16)

            def load_h5l(t):
                if t >= NH5:
                    sp.wait_ge(s_scat[t % NH5], 32 * (t // NH5))
                sp.dma_start(h5l[:, t % NH5], h5_s[t]).then_inc(s_h5l[t % NH5], 16)

            load_gb(0)
            load_x4(0)
            load_x4(1)
            store_h5T(NT - 1)
            for i in range(2):
                sp.wait_ge(s_h5st[i], 16 * NT // 2)
            for n in (36, 37):
                load_half(n, ex_half(n))
            for t in range(4):
                load_h5l(t)
            for t in range(NT):
                store_base(t)
                if t + 2 < NT:
                    load_x4(t + 2)
                if t % TT == TT - 2 and t + 2 < NT:
                    load_gb(t // TT + 1)
                for n in {2: (4, 5), 6: (6, 7), 7: (8, 9), 8: (10, 11), 9: (12, 13), 10: (14, 15)}.get(t, ()):
                    load_h5l(n)
                for n in {0: (8, 9), 1: (10, 11), 4: (12,), 5: (13,), 6: (14,), 7: (15,)}.get(t, ()):
                    load_h5r(n)
                if t in (1, 2):
                    load_half(37 + t, ex_half(37 + t))
            for i in range(NH5):
                sp.wait_ge(s_scat[i], 32 * h5l_uses(i))
            sp.wait_ge(s_dn, NT)
            sp.wait_ge(s_zero, 16 * (2 * NSX - FULL))

            def rows(a, q):
                return a.rearrange("(s p) h -> s p h", p=P)[bass.ds(q, 1)].rearrange("s p h -> (s p) h")

            def load_xs(q, par, wait=None):
                if wait is not None:
                    sp.wait_ge(s_tx, wait)
                sp.dma_start(xsb[:, par], rows(xs_s, q)).then_inc(s_xs[par], 16)

            def store_y(q, par, count):
                sp.wait_ge(s_y4, count)
                sp.dma_start(rows(ys_s, q), ysb[:, par]).then_inc(s_yst[par], 16)

            load_xs(0, 0)
            load_xs(1, 1)
            load_xs(2, 0, 1)
            load_xs(3, 1, 2)
            pairs = sp.value_load(tend[0:1, NE:NE + 1], min_val=NE // 2, max_val=NS // 2)
            with sp.Fori(0, pairs) as i:
                load_xs(i * 2 + 4, 0, i * 2 + 3)
                store_y(i * 2, 0, i * 2 + 1 + AHEAD)
                load_xs(i * 2 + 5, 1, i * 2 + 4)
                store_y(i * 2 + 1, 1, i * 2 + 2 + AHEAD)
            store_y(pairs * 2, 0, pairs * 2 + 1 + AHEAD)
            sp.wait_ge(s_yst[0], pairs * 16 + 32)
            sp.sem_inc(s_end, 1)
            sp.wait_ge(s_yst[1], pairs * 16 + 16)
            sp.sem_inc(s_end, 1)
            for t in range(NT):
                sp.wait_ge(s_o4, t + 1)
                sp.dma_start(out_d[t], g1b[:, t % NG]).then_inc(s_out[t % NG], 16)
            for i in range(NG):
                sp.wait_ge(s_out[i], 16 * (NB + len(range(i, NT, NG))))

        @block.tensor
        def _(pe):
            def modulation(i):
                pe.wait_ge(s_wmod[i], 16)
                for k in range(KT):
                    mm = pe.matmul(mm_ps[i % 4][0:NB, :], cT[:, k, :], wmod[:, i, k, :],
                                   start=k == 0, stop=k == KT - 1)
                mm.then_inc(s_modps, 1)

            def turn(kind, b, tiles=range(TT)):
                for j in tiles:
                    n = hn_count(kind, b, j)
                    pe.wait_ge(s_hn, n)
                    if n > 2:
                        pe.wait_ge(s_hT, n - 2)
                    for k in range(KT):
                        mm = pe.transpose(tp_ps[(n - 1) % 2][:, k, :], hn[:, (n - 1) % 2, k * P:(k + 1) * P],
                                          ident[:, :])
                    mm.then_inc(s_tp, 1)

            def channels_out(s, b, tiles=range(KT)):
                m_ = mix[:, mix_slot(s, b)]
                if b == 0:
                    n = 2 * (w_load_order.index(s) + 1)
                    pe.wait_ge(s_whi, n)
                    pe.wait_ge(s_wlo, n)
                for m in tiles:
                    bank_free(pe, s, b, m)
                    for k in range(KT):
                        if m == 0:
                            pe.wait_ge(s_mhi, split_count(s, b, k))
                            pe.wait_ge(s_mlo, split_count(s, b, k))
                        w = [w_of[s][:, i, k, m * P:(m + 1) * P] for i in range(2)]
                        mm = mm3(pe, mm_ps[m][:, :], w, [m_[:, i, k, :] for i in range(2)],
                                 k == 0, k == KT - 1)
                    mm.then_inc(s_mm, 1)

            def tokens_out(s, b, tiles=range(TT)):
                if b == 0:
                    n = 2 * (w_load_order.index(s) + 1)
                    pe.wait_ge(s_whi, n)
                    pe.wait_ge(s_wlo, n)
                m_ = rw if s == "O" else mix[:, mix_slot(s, b)]
                for j in tiles:
                    bank_free(pe, s, b, j)
                    for k in range(KT):
                        if j == 0:
                            if s == "O":
                                pe.wait_ge(s_rwhi, b * KT + k + 1)
                                pe.wait_ge(s_rwlo, b * KT + k + 1)
                            else:
                                pe.wait_ge(s_mhi, split_count(s, b, k))
                                pe.wait_ge(s_mlo, split_count(s, b, k))
                        a = [m_[:, i, k, j * P:(j + 1) * P] for i in range(2)]
                        mm = mm3(pe, mm_ps[j][:, :], a, [w_of[s][:, i, k, :] for i in range(2)],
                                 k == 0, k == KT - 1)
                    mm.then_inc(s_mm, 1)

            pe.wait_ge(s_const, 2)
            pe.wait_ge(s_csil, 2)
            modulation(0)
            modulation(1)
            modulation(2)
            turn(1, 0, [0, 1])
            modulation(3)
            turn(1, 0, [2, 3])
            pe.wait_ge(s_modsb, 1)
            modulation(4)
            pe.wait_ge(s_modsb, 2)
            modulation(5)
            for b in range(NB):
                if b == 0:
                    pe.wait_ge(s_modsb, 5)
                channels_out("K", b, [0])
                if b == 0:
                    pe.wait_ge(s_modsb, 6)
                channels_out("K", b, [1, 2, 3])
                channels_out("V", b)
                if b:
                    turn(2, b - 1, [0, 1])
                channels_out("R", b, [0])
                if b:
                    turn(2, b - 1, [2, 3])
                channels_out("R", b, [1, 2, 3])
                if b:
                    tokens_out("S", b - 1, [0, 1])
                if b + 1 < NB:
                    turn(1, b + 1, [0, 1])
                if b:
                    tokens_out("S", b - 1, [2])
                if b + 1 < NB:
                    turn(1, b + 1, [2, 3])
                if b:
                    tokens_out("S", b - 1, [3])
                tokens_out("O", b)
            turn(2, NB - 1)
            tokens_out("S", NB - 1)

            def key(g):
                b, m = divmod(g, MF)
                u = 2 * (m // KT)
                if m == 0:
                    if b == 0:
                        pe.wait_ge(s_sr, NT - 2)
                        pe.wait_ge(s_hT, hT_count(2, NB - 1))
                        pe.wait_ge(s_x2, NT)
                        pe.wait_ge(s_sig, NT)
                if b == 0 and m % KT == 0:
                    pe.wait_ge(s_whi, 10 + 2 * (u + 1))
                    pe.wait_ge(s_wlo, 10 + 2 * (u + 1))
                if g >= 2:
                    pe.wait_ge(s_silo, g - 1)
                for k in range(KT):
                    if m == 0:
                        pe.wait_ge(s_xkhi, b * KT + k + 1)
                        pe.wait_ge(s_xklo, b * KT + k + 1)
                    w = [cm_unit(u)[:, i, k, (m % KT) * P:(m % KT + 1) * P] for i in range(2)]
                    mm = mm3(pe, kk_ps[g % 2][:, :], w, [xk[:, i, k, :] for i in range(2)], k == 0, k == KT - 1)
                mm.then_inc(s_kk, 1)

            def value(g):
                b, m = divmod(g, MF)
                u = 2 * (m // KT) + 1
                if b == 0 and m % KT == 0:
                    pe.wait_ge(s_whi, 10 + 2 * (u + 1))
                    pe.wait_ge(s_wlo, 10 + 2 * (u + 1))
                pe.wait_ge(s_sihi, g + 1)
                pe.wait_ge(s_silo, g + 1)
                if g == 0:
                    pe.wait_ge(s_sr, NT)
                for j in range(TT):
                    if m == 0 and b:
                        pe.wait_ge(s_kvr, (b - 1) * TT + j + 1)
                    a = [silu[:, g % NSILU, i, j * P:(j + 1) * P] for i in range(2)]
                    mm = mm3(pe, kv_ps[j][:, :], a, [cm_unit(u)[:, i, m % KT, :] for i in range(2)],
                             m == 0, m == MF - 1)
                mm.then_inc(s_kv, 1)

            def turn5(t):
                pe.wait_ge(s_h5, t + 1)
                if t:
                    pe.wait_ge(s_h5T, t)
                for k in range(KT):
                    mm = pe.transpose(t5_ps[:, k, :], h5b[:, t % 2, k * P:(k + 1) * P], ident[:, :])
                mm.then_inc(s_t5, 1)

            def router(t):
                pe.wait_ge(s_h5T, t + 1)
                for k in range(KT):
                    mm = pe.matmul(rt_ps[:, t, :], h5T[:, t % 2, k, :], wrt[:, k, :], start=k == 0, stop=k == KT - 1)
                mm.then_inc(s_rt, 1)

            for g in range(NB * MF + 2):
                b, m = divmod(g, MF)
                if m == 0 and b:
                    value(g - 2)
                if g < NB * MF:
                    key(g)
                if g >= 2 and m:
                    value(g - 2)
                if b and 4 <= m < 4 + TT:
                    turn5((b - 1) * TT + m - 4)
                if b and 5 <= m < 5 + TT:
                    router((b - 1) * TT + m - 5)
            def shared_up(b, tiles=range(KT)):
                for m in tiles:
                    n = b * KT + m
                    if n >= 2:
                        pe.wait_ge(s_midlo, n - 1)
                    else:
                        pe.wait_ge(s_silo, NB * MF)
                    if n == 0:
                        pe.wait_ge(s_whi, 28)
                        pe.wait_ge(s_wlo, 28)
                    for k in range(KT):
                        if m == 0:
                            pe.wait_ge(s_hthi, b * KT + k + 1)
                            pe.wait_ge(s_htlo, b * KT + k + 1)
                        w = [ex_w[:, 0, i, k * H + m * P:k * H + (m + 1) * P] for i in range(2)]
                        mm = mm3(pe, up_ps[n % 2][:, :], w, [ht[:, i, k, :] for i in range(2)], k == 0, k == KT - 1)
                    mm.then_inc(s_up, 1)

            def shared_down(b, tiles=range(TT)):
                if b == 0 and 0 in tiles:
                    pe.wait_ge(s_whi, 30)
                    pe.wait_ge(s_wlo, 30)
                for j in tiles:
                    t = b * TT + j
                    if t >= 3:
                        pe.wait_ge(s_gsh, t - 2)
                    else:
                        pe.wait_ge(s_kvr, NT)
                    for k in range(KT):
                        if j == 0:
                            pe.wait_ge(s_midhi, b * KT + k + 1)
                            pe.wait_ge(s_midlo, b * KT + k + 1)
                        a = [mid[:, b % 2, i, k, j * P:(j + 1) * P] for i in range(2)]
                        w = [ex_w[:, 1, i, k * H:(k + 1) * H] for i in range(2)]
                        mm = mm3(pe, dn_ps[t % 3][:, :], a, w, k == 0, k == KT - 1)
                    mm.then_inc(s_dn, 1)

            def prefix_sums():
                pe.wait_ge(s_cho, 1)
                pe.wait_ge(s_con, 12)
                c = chosen[:, :, :].rearrange("p t e -> p (t e)")
                pe.matmul(pf_ps[:, 0].rearrange("p t e -> p (t e)"), upper[:, :], c, start=True, stop=True)
                pe.matmul(pf_ps[:, 1].rearrange("p t e -> p (t e)"), onesb[:, :].to_broadcast([P, P]), c, start=True, stop=True)\
                    .then_inc(s_pf, 1)

            last = NT - TT
            shared_up(0)
            turn5(last)
            shared_down(0, [0])
            turn5(last + 1)
            router(last)
            shared_down(0, [1])
            turn5(last + 2)
            router(last + 1)
            shared_down(0, [2])
            shared_up(1, [0])
            turn5(last + 3)
            router(last + 2)
            shared_up(1, [1])
            shared_up(1, [2, 3])
            router(last + 3)
            shared_down(0, [3])
            shared_down(1, [0, 1, 2])
            prefix_sums()
            shared_down(1, [3])
            shared_up(2)
            shared_down(2)
            shared_up(3)
            shared_down(3)

            pe.wait_ge(s_pos, 2)
            pe.wait_ge(s_gsh, NT)

            def turn_x(q, par, xs_count, free_count):
                pe.wait_ge(s_xs[par], xs_count)
                if free_count is not None:
                    pe.wait_ge(s_txhi, free_count)
                    pe.wait_ge(s_txlo, free_count)
                for k in range(KT):
                    mm = pe.transpose(xs_ps[par][:, k, :], xsb[:, par, k * P:(k + 1) * P], ident[:, :])
                mm.then_inc(s_tx, 1)

            def expert_of(q):
                both = pe.value_load(tab[0:1, 0, bass.ds(q, 1)], min_val=0, max_val=8 * NE - 1)
                return both, nc.s_assert_within(
                    both & 7, 0, RING - 1, skip_runtime_bounds_check_because="the low bits are (.. mod RING)")

            def up(word, r, par, count, free_count):
                pe.wait_ge(s_exr, word + 1)
                pe.wait_ge(s_txhi, count)
                pe.wait_ge(s_txlo, count)
                if free_count is not None:
                    pe.wait_ge(s_g4, free_count)
                for k in range(KT):
                    a = [xsT[:, par, i, k, :] for i in range(2)]
                    w = [ex_w[:, bass.ds(r, 1), i, k * (H // 2):(k + 1) * (H // 2)].rearrange("p a c -> p (a c)")
                         for i in range(2)]
                    mm = mm3(pe, up4_ps[par][:, 0:H // 2], a, w, k == 0, k == KT - 1)
                mm.then_inc(s_u4, 1)

            def turn_m(q, par, count, free_count):
                pe.wait_ge(s_g4, count)
                if free_count is not None:
                    pe.wait_ge(s_tmhi, free_count)
                    pe.wait_ge(s_tmlo, free_count)
                for k in range(2):
                    mm = pe.transpose(tm_ps[:, k, :], mb[:, par, k * P:(k + 1) * P], ident[:, :])
                mm.then_inc(s_tm, 1)

            def down(r, par, count, free_count):
                pe.wait_ge(s_tmhi, count)
                pe.wait_ge(s_tmlo, count)
                pe.wait_ge(s_y4, free_count)
                for k in range(2):
                    a = [mbT[:, par, i, k, :] for i in range(2)]
                    w = [ex_w[:, bass.ds(r, 1), i, HALF + k * H:HALF + (k + 1) * H].rearrange("p a c -> p (a c)")
                         for i in range(2)]
                    mm = mm3(pe, dn4_ps[par][:, :], a, w, k == 0, k == 1)
                mm.then_inc(s_d4, 1)

            turn_x(0, 0, 16, None)
            first = expert_of(0)
            up(*first, 0, 1, None)
            turn_x(1, 1, 16, None)
            turn_m(0, 0, 1, None)
            pairs = pe.value_load(tend[0:1, NE:NE + 1], min_val=NE // 2, max_val=NS // 2)
            with pe.Fori(0, pairs) as i:
                e1, r1 = expert_of(i * 2 + 1)
                up(e1, r1, 1, i * 2 + 2, i * 2 + 1)
                turn_x(i * 2 + 2, 0, i * 16 + 32, i * 2 + 1)
                _, r0 = expert_of(i * 2)
                down(r0, 0, i * 2 + 1, i * 2 + 1)
                turn_m(i * 2 + 1, 1, i * 2 + 2, i * 2 + 1)
                e2, r2 = expert_of(i * 2 + 2)
                up(e2, r2, 0, i * 2 + 3, i * 2 + 2)
                turn_x(i * 2 + 3, 1, i * 16 + 32, i * 2 + 2)
                down(r1, 1, i * 2 + 2, i * 2 + 2)
                turn_m(i * 2 + 2, 0, i * 2 + 3, i * 2 + 2)
            _, r = expert_of(pairs * 2)
            down(r, 0, pairs * 2 + 1, pairs * 2 + 1)

        @block.vector
        def _(dve):
            own = Count(s_dve)

            def done(ins):
                dve.wait_ge(s_dve, own.up(ins))

            dve.memset(hT[:, :, 0:1], 0.0).then_inc(s_const, 1)
            dve.wait_ge(s_csil, 1)
            dve.tensor_tensor(cT[:, :, :], cT[:, :, :], sgc[:, :, :], ALU.mult).then_inc(s_csil, 1)

            def variance(src, st, mv, t, kind, s_out):
                j = t % TT
                if t >= TT:
                    dve.wait_ge(s_out, t - TT + 1)
                    dve.wait_ge(s_hn, hn_count(kind, t // TT - 1, j))
                done(dve.bn_stats(st[:, j], src))
                done(dve.bn_aggr(mv[:, j], st[:, j]))
                dve.tensor_scalar(mv[:, j, 1:2], mv[:, j, 1:2], EPS, None, ALU.add).then_inc(s_out, 1)

            def first_norm_a(b, j):
                t = b * TT + j
                dve.wait_ge(s_x[j], 16 * (b + 1))
                variance(xb[:, j], st1, mv1, t, 1, s_st1)

            def first_norm_b(b, j):
                t = b * TT + j
                dve.wait_ge(s_rs1, t + 1)
                done(dve.tensor_scalar(xb[:, j], xb[:, j], mv1[:, j, 0:1], rs1[:, j:j + 1],
                                       ALU.subtract, ALU.mult))
                dve.wait_ge(s_bc, 32 * (b + 1))
                dve.tensor_tensor(xb[:, j], xb[:, j], ca_bc[:, :], ALU.mult).then_inc(s_hca, 1)

            def first_norm_c(b, j):
                t = b * TT + j
                dve.wait_ge(s_h0, t + 1)
                variance(xb[:, j], st2, mv2, t, 1, s_st2)

            def first_norm(b, i):
                if i < TT:
                    first_norm_a(b, i)
                if 1 <= i <= TT:
                    first_norm_b(b, i - 1)
                if i >= 2:
                    first_norm_c(b, i - 2)

            def hn_out(kind, b, tiles=range(TT)):
                src, mv, rs, s_r = (xb, mv2, rs2, s_rs2) if kind == 1 else (x2b, mv3, rs3, s_rs3)
                for j in tiles:
                    t = b * TT + j
                    n = hn_count(kind, b, j)
                    dve.wait_ge(s_r, t + 1)
                    if n > 2:
                        dve.wait_ge(s_tp, n - 2)
                    dve.tensor_scalar(hn[:, (n - 1) % 2], src[:, j], mv[:, j, 0:1], rs[:, j:j + 1],
                                      ALU.subtract, ALU.mult).then_inc(s_hn, 1)

            def differences(kind, b):
                dve.wait_ge(s_hT, hT_count(kind, b))
                for k in range(KT):
                    ins = dve.tensor_tensor(dT[:, k, :], hT[:, k, 1:T + 1], hT[:, k, 0:T], ALU.subtract)
                    ins.then_inc(s_dT, 1)
                dve.wait_ge(s_dT, turns.index((kind, b)) * KT + KT)

            def mixed(s, b, tiles=range(KT)):
                vec = {"K": V_MK, "V": V_MV, "R": V_MR, "X": V_CK, "S": V_CR}[s]
                for k in tiles:
                    n = raw_count(s, b, k)
                    if n > 2:
                        i, kk = divmod(n - 3, KT)
                        s0, b0 = raw_order[i]
                        if s0 == "X":
                            dve.wait_ge(s_xkst[(n - 1) % 2], xk_stored(n - 2))
                        else:
                            dve.wait_ge(s_mhi, split_count(s0, b0, kk))
                            dve.wait_ge(s_mlo, split_count(s0, b0, kk))
                    dve.scalar_tensor_tensor(out=raw[:, (n - 1) % 2], in0=dT[:, k, :], scalar=vecs[:, vec, k:k + 1],
                                             in1=hT[:, k, 0:T], op0=ALU.mult, op1=ALU.add).then_inc(s_raw, 1)

            def k_out(b, tiles):
                for m in tiles:
                    dve.wait_ge(s_kw, b * KT + m + 1)
                    dve.scalar_tensor_tensor(out=eT[:, m, :], in0=eT[:, m, :], scalar=PP0, in1=eT[:, m, :],
                                             op0=ALU.max, op1=ALU.subtract).then_inc(s_ke, 1)

            def v_out(b, tiles):
                for m in tiles:
                    dve.wait_ge(s_e2, b * KT + m + 1)
                    dve.wait_ge(s_mm, mm_count("V", b, m))
                    dve.tensor_tensor(eT[:, m, :], mm_ps[m][:, :], eT[:, m, :], ALU.mult).then_inc(s_vm, 1)

            def r_out(b, tiles):
                for m in tiles:
                    dve.wait_ge(s_sig, b * KT + m + 1)
                    dve.wait_ge(s_va, b * KT + m + 1)
                    dve.tensor_tensor(eT[:, m, :], eT[:, m, :], sig[:, m % 2], ALU.mult).then_inc(s_rw, 1)

            def o_out(b, tiles=range(TT)):
                for j in tiles:
                    t = b * TT + j
                    dve.wait_ge(s_mm, mm_count("O", b, j))
                    dve.wait_ge(s_h0r[t % 2], 16 * (t // 2 + 1))
                    if b:
                        dve.wait_ge(s_x2st[j], 16 * b)
                        dve.wait_ge(s_hn, hn_count(2, b - 1, j))
                    dve.tensor_tensor(x2b[:, j], mm_ps[j][:, :], h0r[:, t % 2], ALU.add).then_inc(s_x2, 1)
                    dve.wait_ge(s_x2, t + 1)
                    variance(x2b[:, j], st3, mv3, t, 2, s_st3)

            for j in range(TT):
                first_norm_a(0, j)
            def modulation(i):
                dve.wait_ge(s_modps, i + 1)
                src = mm_ps[i % 4][0:NB, :]
                if i in (0, 3):
                    ins = dve.tensor_copy(modr[:, i], src)
                elif i in (1, 4):
                    ins = dve.tensor_scalar(modr[:, i], src, 1.0, None, ALU.add)
                else:
                    if i == 5:
                        dve.wait_ge(s_modsb, 3)
                    done(dve.tensor_scalar(modt[:, 0], src, 0.0, 2.0, ALU.is_ge, ALU.mult))
                    done(dve.tensor_scalar(modt[:, 1], src, -1.0, 0.25, ALU.mult, ALU.max))
                    done(dve.tensor_tensor(modt[:, 1], src, modt[:, 1], ALU.max))
                    done(dve.tensor_scalar(modt[:, 0], modt[:, 0], -1.0, None, ALU.add))
                    ins = dve.tensor_tensor(modr[:, i], modt[:, 0], modt[:, 1], ALU.mult)
                ins.then_inc(s_modsb, 1)

            modulation(0)
            modulation(1)
            for j in range(TT + 1):
                if j < TT:
                    first_norm_b(0, j)
                if j:
                    first_norm_c(0, j - 1)
            hn_out(1, 0)
            modulation(2)
            modulation(3)
            differences(1, 0)
            mixed("K", 0, [0, 1])
            modulation(4)
            modulation(5)
            mixed("K", 0, [2, 3])
            mixed("V", 0)
            for b in range(NB):
                more = b + 1 < NB
                for m in range(KT):
                    k_out(b, [m])
                    if more and m < 2:
                        first_norm(b + 1, m)
                mixed("R", b, [0, 1])
                v_out(b, [0])
                mixed("R", b, [2])
                if b:
                    hn_out(2, b - 1, [0, 1])
                v_out(b, [1])
                mixed("R", b, [3])
                if more:
                    first_norm(b + 1, 2)
                v_out(b, [2])
                if b:
                    hn_out(2, b - 1, [2])
                v_out(b, [3])
                if b:
                    hn_out(2, b - 1, [3])
                if more:
                    first_norm(b + 1, 3)
                if b:
                    differences(2, b - 1)
                    mixed("S", b - 1)
                r_out(b, [0, 1])
                if b:
                    mixed("X", b - 1, [0, 1])
                if more:
                    first_norm(b + 1, 4)
                if b:
                    mixed("X", b - 1, [2, 3])
                if more:
                    first_norm(b + 1, 5)
                    hn_out(1, b + 1, [0, 1])
                r_out(b, [2, 3])
                if more:
                    hn_out(1, b + 1, [2, 3])
                    differences(1, b + 1)
                    mixed("K", b + 1)
                    mixed("V", b + 1, [0, 1])
                    o_out(b, [0])
                    mixed("V", b + 1, [2])
                    o_out(b, [1])
                    mixed("V", b + 1, [3])
                    o_out(b, [2, 3])
                else:
                    o_out(b)
            hn_out(2, NB - 1)
            differences(2, NB - 1)
            mixed("S", NB - 1)
            mixed("X", NB - 1)

            def silu_lo(g):
                dve.wait_ge(s_sihi, g + 1)
                dve.tensor_tensor(silu[:, g % NSILU, 1, :], kk_ps[g % 2][:, :], silu[:, g % NSILU, 0, :].bitcast(F32),
                                  ALU.subtract).then_inc(s_silo, 1)

            def post_a(t):
                dve.wait_ge(s_kv, (t // TT + 1) * MF)
                dve.wait_ge(s_lds[t % TT], 16 * (t // TT + 1))
                if t >= TT:
                    dve.wait_ge(s_gx3, t - TT + 1)
                dve.tensor_tensor(x4b[:, t % TT], kv_ps[t % TT][:, :], x4b[:, t % TT], ALU.mult).then_inc(s_kvr, 1)

            def post_b(t):
                dve.wait_ge(s_x3, t + 1)
                dve.wait_ge(s_bc2, 48 * (t // TT + 1))
                dve.tensor_tensor(x4b[:, t % TT], x4b[:, t % TT], bc2[:, 0], ALU.mult).then_inc(s_gx3, 1)

            def post_c(t):
                dve.wait_ge(s_x4, t + 1)
                if t >= 2:
                    dve.wait_ge(s_rs5, t - 1)
                done(dve.bn_stats(st5[:, t % 2], x4b[:, t % TT]))
                done(dve.bn_aggr(mv5[:, t % 2], st5[:, t % 2]))
                dve.tensor_scalar(mv5[:, t % 2, 1:2], mv5[:, t % 2, 1:2], EPS, None, ALU.add).then_inc(s_st5, 1)

            def post_d(t):
                dve.wait_ge(s_rs5, t + 1)
                if t >= 2:
                    dve.wait_ge(s_h5st[t % 2], 16 * (t // 2))
                    dve.wait_ge(s_t5, t - 1)
                done(dve.tensor_scalar(h5b[:, t % 2], x4b[:, t % TT], mv5[:, t % 2, 0:1], rs5[:, t % 2:t % 2 + 1],
                                       ALU.subtract, ALU.mult))
                dve.tensor_tensor(h5b[:, t % 2], h5b[:, t % 2], bc2[:, 1], ALU.mult).then_inc(s_hcb, 1)

            def xk_lo(b, tiles):
                for k in tiles:
                    n = b * KT + k
                    dve.wait_ge(s_xkhi, n + 1)
                    dve.tensor_tensor(xk[:, 1, k, :], xkr[:, n % 2], xk[:, 0, k, :].bitcast(F32), ALU.subtract)\
                        .then_inc(s_xklo, 1)

            for g in range(NB * MF):
                b, m = divmod(g, MF)
                if m == MF - 1 and b + 1 < NB:
                    xk_lo(b + 1, [0, 1])
                silu_lo(g)
                if m == MF - 1 and b + 1 < NB:
                    xk_lo(b + 1, [2, 3])
                if b and m == 1:
                    for j in range(TT):
                        post_a((b - 1) * TT + j)
                if b and 1 <= m < 1 + TT:
                    post_b((b - 1) * TT + m - 1)
                if b and 2 <= m < 2 + TT:
                    t = (b - 1) * TT + m - 2
                    post_c(t)
                    post_d(t)
            def weight_lo(n):
                w = ex_w[:, (n - 26) // 2, :, (n % 2) * HALF:(n % 2 + 1) * HALF]
                dve.wait_ge(s_whi, n + 1)
                dve.tensor_tensor(w[:, 1], stage[:, n % 2], w[:, 0].bitcast(F32), ALU.subtract).then_inc(s_wlo, 1)

            def ht_lo(b, tiles):
                for k in tiles:
                    n = b * KT + k
                    dve.wait_ge(s_hthi, n + 1)
                    dve.tensor_tensor(ht[:, 1, k, :], h5r[:, n % 2], ht[:, 0, k, :].bitcast(F32), ALU.subtract)\
                        .then_inc(s_htlo, 1)

            def mid_lo(n):
                b, m = divmod(n, KT)
                dve.wait_ge(s_midhi, n + 1)
                dve.tensor_tensor(mid[:, b % 2, 1, m, :], up_ps[n % 2][:, :], mid[:, b % 2, 0, m, :].bitcast(F32),
                                  ALU.subtract).then_inc(s_midlo, 1)

            def gb_shared(t):
                dve.wait_ge(s_dn, t + 1)
                dve.wait_ge(s_gb, 16 * (t // TT + 1))
                if t >= 2:
                    dve.wait_ge(s_basest[t % 2], 16 * (t // 2))
                dve.tensor_tensor(yb[:, t % 2], dn_ps[t % 3][:, :], gb_bc[:, :], ALU.mult).then_inc(s_gsh, 1)
                dve.wait_ge(s_gsh, t + 1)
                dve.wait_ge(s_x4l[t % 2], 16 * (t // 2 + 1))
                dve.tensor_tensor(yb[:, t % 2], yb[:, t % 2], x4l[:, t % 2], ALU.add).then_inc(s_base, 1)

            def per_token(v):
                return v.rearrange("p (t a) -> p t a", a=1).to_broadcast([P, NT, NE])

            def per_expert(v):
                return v.rearrange("p (a e) -> p a e", a=1).to_broadcast([P, NT, NE])

            def choose(c):
                g = gates[:, c, :]
                done(dve.tensor_reduce(g, pr[:, :, :], AX.X, ALU.max))
                done(dve.tensor_tensor(tmp[:, :, :], pr[:, :, :], per_token(g), ALU.is_equal))
                done(dve.tensor_tensor(tmp[:, :, :], tmp[:, :, :], per_expert(rev[:, :]), ALU.mult))
                done(dve.tensor_reduce(red[:, :], tmp[:, :, :], AX.X, ALU.max))
                done(dve.tensor_tensor(oh[:, c], per_expert(rev[:, :]), per_token(red[:, :]), ALU.is_equal))

            def route_a():
                dve.wait_ge(s_con, 12)
                dve.wait_ge(s_rt, NT)
                for i in range(2):
                    dve.wait_ge(s_h5Tst[i], 16 * NT // 2)
                done(dve.tensor_copy(lg[:, :, :], rt_ps[:, :, :]))
                done(dve.tensor_reduce(red[:, :], lg[:, :, :], AX.X, ALU.max))
                dve.tensor_tensor(lg[:, :, :], lg[:, :, :], per_token(red[:, :]), ALU.subtract).then_inc(s_sub, 1)

            def route_b():
                dve.wait_ge(s_exp, 1)
                done(dve.tensor_reduce(red[:, :], pr[:, :, :], AX.X, ALU.add))
                done(dve.reciprocal(red2[:, :], red[:, :]))
                done(dve.tensor_tensor(pr[:, :, :], pr[:, :, :], per_token(red2[:, :]), ALU.mult))

            def route_c():
                done(dve.scalar_tensor_tensor(out=pr[:, :, :], in0=oh[:, 0], scalar=-2.0, in1=pr[:, :, :],
                                              op0=ALU.mult, op1=ALU.add))
                choose(1)
                dve.tensor_tensor(chosen[:, :, :], oh[:, 0], oh[:, 1], ALU.add).then_inc(s_cho, 1)

            def place_a():
                dve.wait_ge(s_pf, 1)
                done(dve.memset(off[:, 0, :], 0.0))
                for t in range(NT):
                    done(dve.tensor_tensor(off[:, t + 1, :], off[:, t, :], pf_ps[:, 1, t, :], ALU.add))

            def place_b():
                count = off[:, NT, :]
                done(dve.tensor_tensor(tmp[:, 0:NE, :], count.rearrange("p (e a) -> p e a", a=1)
                                       .to_broadcast([P, NE, NE]),
                                       thr[:, :].rearrange("p (a k) -> p a k", a=1).to_broadcast([P, NE, NE]),
                                       ALU.is_gt))
                done(dve.tensor_reduce(ntile[:, :], tmp[:, 0:NE, :], AX.X, ALU.add))
                done(dve.tensor_tensor_scan(tends[:, :], ones16[:, :].to_broadcast([P, NE]), ntile[:, :], 0.0, ALU.mult, ALU.add))
                done(dve.tensor_tensor(ntile[:, :], tends[:, :], ntile[:, :], ALU.subtract))
                done(dve.tensor_scalar(ntile[:, :], ntile[:, :], float(P), None, ALU.mult))
                done(dve.tensor_tensor(off[:, 0:NT, :], off[:, 0:NT, :], per_expert(ntile[:, :]), ALU.add))
                done(dve.tensor_tensor(off[:, 0:NT, :], off[:, 0:NT, :], pf_ps[:, 0], ALU.add))

            def place_c():
                for c in range(2):
                    done(dve.tensor_tensor(tmp[:, :, :], off[:, 0:NT, :], oh[:, c], ALU.mult))
                    done(dve.tensor_reduce(red[:, :], tmp[:, :, :], AX.X, ALU.add))
                    ins = dve.tensor_copy(pos[:, c, :], red[:, :])
                    if c == 0:
                        done(ins)
                    else:
                        ins.then_inc(s_pos, 1)

            def place_d():
                done(dve.tensor_tensor(cmp[:, :, :],
                                       tends[0:1, :].rearrange("p (a e) -> p a e", a=1).to_broadcast([1, NSX, NE]),
                                       sidx[:, :].rearrange("p (s a) -> p s a", a=1).to_broadcast([1, NSX, NE]),
                                       ALU.is_le))
                done(dve.tensor_reduce(tabf[:, 0], cmp[:, :, :], AX.X, ALU.add))
                done(dve.tensor_scalar(tabf[:, 0], tabf[:, 0], float(NE - 1), None, ALU.min))
                done(dve.tensor_scalar(tabf[:, 1], tabf[:, 0], float(BASE), None, ALU.add))
                for r in range(RING, NE - 1 + BASE + 1, RING):
                    done(dve.tensor_scalar(tabf[:, 2], tabf[:, 0], float(r - BASE), float(-RING), ALU.is_ge, ALU.mult))
                    done(dve.tensor_tensor(tabf[:, 1], tabf[:, 1], tabf[:, 2], ALU.add))
                done(dve.scalar_tensor_tensor(out=tabf[:, 1], in0=tabf[:, 0], scalar=8.0, in1=tabf[:, 1],
                                              op0=ALU.mult, op1=ALU.add))
                done(dve.tensor_copy(tab[:, 0], tabf[:, 1]))
                done(dve.tensor_copy(tend[:, 0:NE], tends[0:1, :]))
                done(dve.tensor_reduce(tabf[:, 3, 0:1], thr2(), AX.X, ALU.add))
                dve.tensor_copy(tend[:, NE:NE + 1], tabf[:, 3, 0:1]).then_inc(s_pos, 1)

            def thr2():
                done(dve.tensor_scalar(tabf[:, 2, :], sidx[:, :], 2.0, 1.0, ALU.mult, ALU.add))
                done(dve.tensor_scalar(tabf[:, 2, :], tabf[:, 2, :], tends[0:1, NE - 1:NE], None, ALU.is_lt))
                return tabf[:, 2, :]

            for j in range(TT):
                post_a(NT - TT + j)
            t = NT - TT
            post_b(t)
            mid_lo(0)
            post_b(t + 1)
            mid_lo(1)
            post_c(t)
            post_d(t)
            for i in (2, 3):
                mid_lo(i)
                post_b(t + i)
                post_c(t + i - 1)
                post_d(t + i - 1)
            post_c(t + 3)
            post_d(t + 3)
            gb_shared(0)
            dve.wait_ge(s_wlo, 34)
            weight_lo(34)
            weight_lo(35)
            gb_shared(1)
            for m in range(KT):
                mid_lo(KT + m)
            route_a()
            route_b()
            choose(0)
            gb_shared(2)
            weight_lo(36)
            ht_lo(2, [0, 1])
            gb_shared(3)
            route_c()
            weight_lo(37)
            gb_shared(4)
            ht_lo(2, [2, 3])
            place_a()
            gb_shared(5)
            place_b()
            gb_shared(6)
            place_c()
            mid_lo(8)
            gb_shared(7)
            mid_lo(9)
            weight_lo(38)
            weight_lo(39)
            place_d()
            mid_lo(10)
            mid_lo(11)
            gb_shared(8)
            ht_lo(3, [0, 1])
            gb_shared(9)
            ht_lo(3, [2, 3])
            mid_lo(12)
            gb_shared(10)
            mid_lo(13)
            gb_shared(11)
            mid_lo(14)
            mid_lo(15)
            for t in range(3 * TT, NT):
                gb_shared(t)

            def turned_lo(par, count):
                dve.wait_ge(s_txhi, count)
                dve.tensor_tensor(xsT[:, par, 1], xs_ps[par][:, :, :], xsT[:, par, 0].bitcast(F32), ALU.subtract)\
                    .then_inc(s_txlo, 1)

            def turned_mid_lo(par, count):
                dve.wait_ge(s_tmhi, count)
                dve.tensor_tensor(mbT[:, par, 1], tm_ps[:, 0:2, :], mbT[:, par, 0].bitcast(F32), ALU.subtract)\
                    .then_inc(s_tmlo, 1)

            def y_out(par, count, stored):
                dve.wait_ge(s_d4, count)
                if stored is not None:
                    dve.wait_ge(s_yst[par], stored)
                dve.tensor_copy(ysb[:, par], dn4_ps[par][:, :]).then_inc(s_y4, 1)

            dve.sem_inc(s_y4, AHEAD)
            dve.sem_inc(s_yst[1], 16)
            dve.sem_inc(s_yst[0], 16)
            turned_lo(0, 1)
            turned_lo(1, 2)
            turned_mid_lo(0, 1)
            pairs = dve.value_load(tend[0:1, NE:NE + 1], min_val=NE // 2, max_val=NS // 2)
            with dve.Fori(0, pairs) as i:
                turned_lo(0, i * 2 + 3)
                y_out(0, i * 2 + 1, i * 16 + 16)
                turned_mid_lo(1, i * 2 + 2)
                turned_lo(1, i * 2 + 4)
                y_out(1, i * 2 + 2, i * 16 + 16)
                turned_mid_lo(0, i * 2 + 3)
            y_out(0, pairs * 2 + 1, pairs * 16 + 16)

            for t in range(NT):
                b = t // TT
                dve.wait_ge(s_o1, t + 1)
                done(dve.scalar_tensor_tensor(out=g1b[:, t % NG], in0=g2b[:, t % NG], scalar=gates[:, 1, t:t + 1],
                                              in1=g1b[:, t % NG], op0=ALU.mult, op1=ALU.add))
                dve.wait_ge(s_bsl, 16 * (NT + NB))
                done(dve.tensor_tensor(g1b[:, t % NG], g1b[:, t % NG], gb2[:, b], ALU.mult))
                dve.wait_ge(s_bsl, 16 * (NT + NB))
                dve.tensor_tensor(g1b[:, t % NG], g1b[:, t % NG], bsb[:, t], ALU.add).then_inc(s_o4, 1)

        @block.scalar
        def _(act):
            act.wait_ge(s_small, 48)
            act.activation(sgc[:, :, :], cT[:, :, :], ACT.Sigmoid).then_inc(s_csil, 1)

            def weight_hi(n):
                act.wait_ge(s_stage[n % 2], 16 * (n // 2 + 1))
                if n < 10:
                    w = w_of[w_load_order[n // 2]]
                elif n >= 26:
                    u = (n - 26) // 2
                    w = ex_w[:, u].rearrange("p i (k c) -> p i k c", c=H)
                    act.wait_ge(*ex_free()[u])
                else:
                    w = cm_unit((n - 10) // 2)
                    act.wait_ge(s_mm, cm_free()[(n - 10) // 2])
                k0 = (n % 2) * KT // 2
                act.activation(w[:, 0, k0:k0 + KT // 2, :], stage[:, n % 2].rearrange("p (k c) -> p k c", c=H),
                               ACT.Copy).then_inc(s_whi, 1)

            def to_hT(kind, b, tiles=range(TT)):
                g, o = (V_G1, V_B1) if kind == 1 else (V_G2, V_B2)
                i = turns.index((kind, b))
                if i:
                    k0, b0 = turns[i - 1]
                    last = ("R", b0) if k0 == 1 else ("X", b0)
                    act.wait_ge(s_raw, raw_count(*last, KT - 1))
                for j in tiles:
                    n = hn_count(kind, b, j)
                    act.wait_ge(s_tp, n)
                    for k in range(KT):
                        ins = act.activation(hT[:, k, 1 + j * P:1 + (j + 1) * P], tp_ps[(n - 1) % 2][:, k, :],
                                             ACT.Identity, scale=vecs[:, g, k:k + 1], bias=vecs[:, o, k:k + 1])
                    ins.then_inc(s_hT, 1)

            def mixed_hi(s, b, tiles=range(KT)):
                i = split_order.index((s, b))
                for k in tiles:
                    act.wait_ge(s_raw, raw_count(s, b, k))
                    if i >= 2 and k == 0:
                        act.wait_ge(s_mm, mm_count(*split_order[i - 2], 3))
                    act.activation(mix[:, i % 2, 0, k, :], raw[:, (raw_count(s, b, k) - 1) % 2], ACT.Copy)\
                        .then_inc(s_mhi, 1)

            def w_out(b, tiles):
                for m in tiles:
                    act.wait_ge(s_mm, mm_count("K", b, m))
                    if b:
                        act.wait_ge(s_rwlo, (b - 1) * KT + m + 1)
                    act.activation(eT[:, m, :], mm_ps[m][:, :], ACT.Identity, bias=vecs[:, V_FIRST, m:m + 1])\
                        .then_inc(s_kw, 1)

            def exps(b, tiles):
                for m in tiles:
                    n = b * KT + m
                    act.wait_ge(s_ke, n + 1)
                    if n >= 2:
                        act.wait_ge(s_va, n - 1)
                    act.activation(rec[:, m % 2], eT[:, m, :], ACT.Exp).then_inc(s_rec, 1)
                    act.wait_ge(s_rec, n + 1)
                    act.activation(eT[:, m, :], eT[:, m, :], ACT.Exp, scale=-1.0).then_inc(s_e2, 1)

            def sigmoids(b, tiles):
                for m in tiles:
                    n = b * KT + m
                    act.wait_ge(s_mm, mm_count("R", b, m))
                    if n >= 2:
                        act.wait_ge(s_rw, n - 1)
                    act.activation(sig[:, m % 2], mm_ps[m][:, :], ACT.Sigmoid).then_inc(s_sig, 1)

            def rw_hi(b, m):
                act.wait_ge(s_rw, b * KT + m + 1)
                if m == 0:
                    if b:
                        act.wait_ge(s_mm, mm_count("O", b - 1, 3))
                    else:
                        act.wait_ge(s_modst, 16 * 6)
                act.activation(rw[:, 0, m, :], eT[:, m, :], ACT.Copy).then_inc(s_rwhi, 1)

            def sr_out(b, tiles=range(TT)):
                for j in tiles:
                    t = b * TT + j
                    act.wait_ge(s_mm, mm_count("S", b, j))
                    if t >= 2:
                        act.wait_ge(s_srst[t % 2], 16 * (t // 2))
                    act.activation(srb[:, t % 2], mm_ps[j][:, :], ACT.Sigmoid).then_inc(s_sr, 1)

            weight_hi(0)
            weight_hi(1)
            to_hT(1, 0)
            mixed_hi("K", 0)
            weight_hi(2)
            weight_hi(3)
            mixed_hi("V", 0)
            weight_hi(4)
            weight_hi(5)
            for b in range(NB):
                w_out(b, [0, 1])
                exps(b, [0])
                w_out(b, [2])
                exps(b, [1])
                w_out(b, [3])
                mixed_hi("R", b, [0, 1])
                exps(b, [2])
                mixed_hi("R", b, [2])
                exps(b, [3])
                mixed_hi("R", b, [3])
                if b == 0:
                    weight_hi(6)
                    weight_hi(7)
                if b:
                    to_hT(2, b - 1)
                sigmoids(b, [0, 1])
                if b:
                    mixed_hi("S", b - 1)
                rw_hi(b, 0)
                rw_hi(b, 1)
                sigmoids(b, [2, 3])
                rw_hi(b, 2)
                rw_hi(b, 3)
                if b:
                    sr_out(b - 1, [0, 1])
                if b + 1 < NB:
                    to_hT(1, b + 1, [0, 1])
                if b:
                    sr_out(b - 1, [2])
                if b + 1 < NB:
                    to_hT(1, b + 1, [2, 3])
                if b:
                    sr_out(b - 1, [3])
                if b == 0:
                    weight_hi(8)
                    weight_hi(9)
                if b + 1 < NB:
                    mixed_hi("K", b + 1)
                    mixed_hi("V", b + 1)
                else:
                    weight_hi(10)
                    weight_hi(11)
            to_hT(2, NB - 1)
            mixed_hi("S", NB - 1)
            weight_hi(12)
            weight_hi(13)

            def xk_hi(b, tiles=range(KT)):
                for k in tiles:
                    n = b * KT + k
                    act.wait_ge(s_xkr[n % 2], 16 * (n // 2 + 1))
                    if b:
                        act.wait_ge(s_kk, b * MF)
                    act.activation(xk[:, 0, k, :], xkr[:, n % 2], ACT.Copy).then_inc(s_xkhi, 1)

            def silu_hi(g):
                act.wait_ge(s_kk, g + 1)
                act.activation(kk_ps[g % 2][:, :], kk_ps[g % 2][:, :], ACT.Silu).then_inc(s_silu, 1)
                act.wait_ge(s_silu, g + 1)
                if g >= NSILU:
                    act.wait_ge(s_kv, g - NSILU + 1)
                act.activation(silu[:, g % NSILU, 0, :], kk_ps[g % 2][:, :], ACT.Copy).then_inc(s_sihi, 1)

            def to_h5T(t):
                act.wait_ge(s_t5, t + 1)
                if t >= 2:
                    act.wait_ge(s_h5Tst[t % 2], 16 * (t // 2))
                    act.wait_ge(s_rt, t - 1)
                act.activation(h5T[:, t % 2], t5_ps[:, :, :], ACT.Copy).then_inc(s_h5T, 1)

            def ht_hi(b, tiles=range(KT)):
                for k in tiles:
                    n = b * KT + k
                    act.wait_ge(s_h5r[n % 2], 16 * (n // 2 + 1))
                    if n == 0:
                        act.wait_ge(s_kk, (NB - 1) * MF + 12)
                    if b:
                        act.wait_ge(s_up, b * KT)
                    act.activation(ht[:, 0, k, :], h5r[:, n % 2], ACT.Copy).then_inc(s_hthi, 1)

            act.wait_ge(s_raw, raw_count("X", NB - 1, KT - 1))
            xk_hi(0, [0, 1])
            sr_out(NB - 1, [0, 1])
            xk_hi(0, [2, 3])
            sr_out(NB - 1, [2, 3])
            weight_hi(14)
            weight_hi(15)
            for g in range(NB * MF):
                b, m = divmod(g, MF)
                if m == MF - 1 and b + 1 < NB:
                    xk_hi(b + 1, [0, 1])
                silu_hi(g)
                if g < 5:
                    weight_hi(16 + 2 * g)
                    weight_hi(17 + 2 * g)
                if b and 4 <= m < 4 + TT:
                    to_h5T((b - 1) * TT + m - 4)
                if m == MF - 1 and b + 1 < NB:
                    xk_hi(b + 1, [2, 3])
                if b == NB - 1 and m >= 6 and m % 2 == 0 and m < 14:
                    weight_hi(20 + m)
                    weight_hi(21 + m)
                if b == NB - 1 and m >= 12:
                    ht_hi(0, [m - 12])

            def gelu(b, tiles=range(KT)):
                for m in tiles:
                    n = b * KT + m
                    act.wait_ge(s_up, n + 1)
                    act.activation(up_ps[n % 2][:, :], up_ps[n % 2][:, :], ACT.Gelu).then_inc(s_gelu, 1)
                    act.wait_ge(s_gelu, n + 1)
                    if b == 0 and m == 0:
                        act.wait_ge(s_kv, NB * MF)
                    if b >= 2:
                        act.wait_ge(s_dn, (b - 1) * TT)
                    act.activation(mid[:, b % 2, 0, m, :], up_ps[n % 2][:, :], ACT.Copy).then_inc(s_midhi, 1)

            gelu(0)
            to_h5T(NT - 4)
            ht_hi(1, [0, 1])
            to_h5T(NT - 3)
            ht_hi(1, [2, 3])
            to_h5T(NT - 2)
            weight_hi(34)
            weight_hi(35)
            gelu(1, [0])
            to_h5T(NT - 1)
            gelu(1, [1])
            gelu(1, [2, 3])
            weight_hi(36)
            act.wait_ge(s_sub, 1)
            act.activation(pr[:, :, :], lg[:, :, :], ACT.Exp).then_inc(s_exp, 1)
            weight_hi(37)
            ht_hi(2)
            weight_hi(38)
            gelu(2, [0])
            weight_hi(39)
            gelu(2, [1, 2, 3])
            ht_hi(3)
            gelu(3)

            def turned_hi(par, count):
                act.wait_ge(s_tx, count)
                act.activation(xsT[:, par, 0], xs_ps[par][:, :, :], ACT.Copy).then_inc(s_txhi, 1)

            def gelu4(par, count):
                act.wait_ge(s_u4, count)
                act.activation(mb[:, par], up4_ps[par][:, 0:H // 2], ACT.Gelu).then_inc(s_g4, 1)

            def turned_mid_hi(par, count):
                act.wait_ge(s_tm, count)
                act.activation(mbT[:, par, 0], tm_ps[:, 0:2, :], ACT.Copy).then_inc(s_tmhi, 1)

            turned_hi(0, 1)
            gelu4(0, 1)
            turned_hi(1, 2)
            turned_mid_hi(0, 1)
            pairs = act.value_load(tend[0:1, NE:NE + 1], min_val=NE // 2, max_val=NS // 2)
            with act.Fori(0, pairs) as i:
                gelu4(1, i * 2 + 2)
                turned_hi(0, i * 2 + 3)
                turned_mid_hi(1, i * 2 + 2)
                gelu4(0, i * 2 + 3)
                turned_hi(1, i * 2 + 4)
                turned_mid_hi(0, i * 2 + 3)

            for t in range(NT):
                act.wait_ge(s_scat[t % NG], 32 * (h5l_uses(t % NG) + t // NG + 1))
                act.activation(g1b[:, t % NG], g1b[:, t % NG], ACT.Copy, scale=gates[:, 0, t:t + 1]).then_inc(s_o1, 1)

        @block.gpsimd
        def _(pool):
            pool.memset(ident[:, :], 0.0).then_inc(s_id, 1)
            pool.wait_ge(s_id, 1)
            pool.affine_select(out=ident[:, :], in_=ident[:, :], compare_op=ALU.not_equal, fill=1.0, base=0,
                               pattern=[[-1, P]], channel_multiplier=1).then_inc(s_const, 1)
            pool.memset(zero[:, :], 0.0).then_inc(s_con, 1)
            pool.memset(onesb[:, :], 1.0).then_inc(s_con, 1)
            pool.memset(upper[:, :], 1.0).then_inc(s_con, 1)
            pool.memset(ones16[:, :], 1.0).then_inc(s_con, 1)
            pool.iota(iot[:, 0:NE], [[128, NE]], base=0, channel_multiplier=0).then_inc(s_con, 1)
            pool.wait_ge(s_con, 5)
            pool.tensor_copy(thr[:, :], iot[:, 0:NE]).then_inc(s_con, 1)
            pool.affine_select(out=upper[:, :], in_=upper[:, :], compare_op=ALU.is_gt, fill=0.0, base=0,
                               pattern=[[1, P]], channel_multiplier=-1).then_inc(s_con, 1)
            pool.wait_ge(s_con, 7)
            pool.memset(thr[:, 0:1], -1.0).then_inc(s_con, 1)
            pool.iota(iot[:, 0:NE], [[-1, NE]], base=NE, channel_multiplier=0).then_inc(s_con, 1)
            pool.wait_ge(s_con, 9)
            pool.tensor_copy(rev[:, :], iot[:, 0:NE]).then_inc(s_con, 1)
            pool.wait_ge(s_con, 10)
            pool.iota(iot[:, :], [[1, NSX]], base=0, channel_multiplier=0).then_inc(s_con, 1)
            pool.wait_ge(s_con, 11)
            pool.tensor_copy(sidx[:, :], iot[0:1, :]).then_inc(s_con, 1)
            pool.memset(neghalf[:, :], -0.5).then_inc(s_id, 1)
            pool.wait_ge(s_id, 2)

            def weight_lo(n):
                if n < 10:
                    w = w_of[w_load_order[n // 2]]
                elif n < 26:
                    w = cm_unit((n - 10) // 2)
                else:
                    w = ex_w[:, (n - 26) // 2].rearrange("p i (k c) -> p i k c", c=H)
                k0 = (n % 2) * KT // 2
                pool.wait_ge(s_whi, n + 1)
                pool.tensor_tensor(w[:, 1, k0:k0 + KT // 2, :], stage[:, n % 2].rearrange("p (k c) -> p k c", c=H),
                                   w[:, 0, k0:k0 + KT // 2, :].bitcast(F32), ALU.subtract).then_inc(s_wlo, 1)

            def rsqrt(rs, mv, b, j, s_in, s_out):
                pool.wait_ge(s_in, b * TT + j + 1)
                pool.tensor_tensor(rs[:, j:j + 1], mv[:, j, 1:2], neghalf[:, :], ALU.pow).then_inc(s_out, 1)

            def h0_out(b, j):
                pool.wait_ge(s_hca, b * TT + j + 1)
                pool.tensor_tensor(xb[:, j], xb[:, j], sa_bc[:, :], ALU.add).then_inc(s_h0, 1)

            def first_norm(b, i):
                if i < TT:
                    rsqrt(rs1, mv1, b, i, s_st1, s_rs1)
                if 1 <= i <= TT:
                    h0_out(b, i - 1)
                if i >= 2:
                    rsqrt(rs2, mv2, b, i - 2, s_st2, s_rs2)

            def wkv(b, tiles):
                for m in tiles:
                    pool.wait_ge(s_vm, b * KT + m + 1)
                    pool.tensor_tensor(eT[:, m, :], eT[:, m, :], rec[:, m % 2], ALU.mult).then_inc(s_va, 1)

            def rw_lo(b, m):
                pool.wait_ge(s_rwhi, b * KT + m + 1)
                pool.tensor_tensor(rw[:, 1, m, :], eT[:, m, :], rw[:, 0, m, :].bitcast(F32), ALU.subtract)\
                    .then_inc(s_rwlo, 1)

            def mixed_lo(s, b, tiles=range(KT)):
                i = split_order.index((s, b))
                for k in tiles:
                    pool.wait_ge(s_mhi, split_count(s, b, k))
                    pool.tensor_tensor(mix[:, i % 2, 1, k, :], raw[:, (raw_count(s, b, k) - 1) % 2],
                                       mix[:, i % 2, 0, k, :].bitcast(F32), ALU.subtract).then_inc(s_mlo, 1)

            for j in range(TT):
                rsqrt(rs1, mv1, 0, j, s_st1, s_rs1)
            weight_lo(0)
            weight_lo(1)
            for i in range(1, TT + 2):
                if i <= TT:
                    h0_out(0, i - 1)
                if i >= 2:
                    rsqrt(rs2, mv2, 0, i - 2, s_st2, s_rs2)
            mixed_lo("K", 0)
            weight_lo(2)
            weight_lo(3)
            mixed_lo("V", 0)
            weight_lo(4)
            weight_lo(5)
            for b in range(NB):
                more = b + 1 < NB
                for i in (0, 1) if more else ():
                    first_norm(b + 1, i)
                mixed_lo("R", b, [0, 1])
                wkv(b, [0])
                mixed_lo("R", b, [2])
                wkv(b, [1])
                mixed_lo("R", b, [3])
                if more:
                    first_norm(b + 1, 2)
                wkv(b, [2, 3])
                if more:
                    first_norm(b + 1, 3)
                if b:
                    mixed_lo("S", b - 1)
                rw_lo(b, 0)
                rw_lo(b, 1)
                for i in (4, 5) if more else ():
                    first_norm(b + 1, i)
                if b == 0:
                    weight_lo(6)
                    weight_lo(7)
                rw_lo(b, 2)
                rw_lo(b, 3)
                if b == 0:
                    weight_lo(8)
                    weight_lo(9)
                if more:
                    mixed_lo("K", b + 1)
                    mixed_lo("V", b + 1)
                else:
                    weight_lo(10)
                    weight_lo(11)
                for j in range(TT):
                    rsqrt(rs3, mv3, b, j, s_st3, s_rs3)
            mixed_lo("S", NB - 1)
            weight_lo(12)
            weight_lo(13)

            def first_xk_lo():
                for k in range(KT):
                    pool.wait_ge(s_xkhi, k + 1)
                    pool.tensor_tensor(xk[:, 1, k, :], xkr[:, k % 2], xk[:, 0, k, :].bitcast(F32), ALU.subtract)\
                        .then_inc(s_xklo, 1)

            def post(t):
                pool.wait_ge(s_kvr, t + 1)
                pool.wait_ge(s_ld[t % 2], 32 * (t // 2 + 1))
                pool.tensor_tensor(x4b[:, t % TT], x4b[:, t % TT], ld[:, t % 2, 0], ALU.add).then_inc(s_x3, 1)
                pool.wait_ge(s_gx3, t + 1)
                pool.tensor_tensor(x4b[:, t % TT], x4b[:, t % TT], ld[:, t % 2, 1], ALU.add).then_inc(s_x4, 1)

            def post_norm(t):
                pool.wait_ge(s_st5, t + 1)
                if t >= 2:
                    pool.wait_ge(s_hcb, t - 1)
                pool.tensor_tensor(rs5[:, t % 2:t % 2 + 1], mv5[:, t % 2, 1:2], neghalf[:, :], ALU.pow)\
                    .then_inc(s_rs5, 1)
                pool.wait_ge(s_hcb, t + 1)
                pool.tensor_tensor(h5b[:, t % 2], h5b[:, t % 2], bc2[:, 2], ALU.add).then_inc(s_h5, 1)

            def posts(b):
                for i in range(TT + 1):
                    if i < TT:
                        post(b * TT + i)
                    if i:
                        post_norm(b * TT + i - 1)

            first_xk_lo()
            for n in range(14, 18):
                weight_lo(n)
            for n in range(18, 26):
                weight_lo(n)
            for b in range(NB - 1):
                posts(b)
            for n in range(26, 34):
                weight_lo(n)

            def ht_lo(b):
                for k in range(KT):
                    n = b * KT + k
                    pool.wait_ge(s_hthi, n + 1)
                    pool.tensor_tensor(ht[:, 1, k, :], h5r[:, n % 2], ht[:, 0, k, :].bitcast(F32), ALU.subtract)\
                        .then_inc(s_htlo, 1)

            def scatter(t):
                pool.wait_ge(s_h5l[t % NH5], 16 * (t // NH5 + 1))
                for c in range(2):
                    pool.indirect_dma_start(xs_s, bass.IndirectOffsetOnAxis(ap=pos[:, c, t:t + 1], axis=0),
                                            h5l[:, t % NH5], None).then_inc(s_scat[t % NH5], 16)

            ht_lo(0)
            posts(NB - 1)
            ht_lo(1)
            def expert_load(n):
                if n >= 2:
                    pool.wait_ge(s_exd, 2 * (n - 1))
                e = PRE + n // 2
                pool.dma_start(stage[:, n % 2], wex_d[2 + e, :, (n % 2) * HALF:(n % 2 + 1) * HALF])\
                    .then_inc(s_exs[n % 2], 16)

            def expert_split(n):
                e = PRE + n // 2
                pool.wait_ge(s_exs[n % 2], 16 * (n // 2 + 1))
                if n % 2 == 0:
                    if e < RING:
                        pool.wait_ge(s_dn, NT)
                    else:
                        end = pool.value_load(tend[0:1, e - RING:e - RING + 1], min_val=1, max_val=NS)
                        pool.wait_ge(s_d4, end)
                half = slice((n % 2) * HALF, (n % 2 + 1) * HALF)
                hi, lo = (ex_w[:, ring_slot(e), i, half] for i in range(2))
                pool.tensor_tensor(hi, stage[:, n % 2], zero[:, 0:1].to_broadcast([P, HALF]), ALU.add).then_inc(s_exd, 1)
                pool.wait_ge(s_exd, 2 * n + 1)
                pool.tensor_tensor(lo, stage[:, n % 2], hi.bitcast(F32), ALU.subtract).then_inc(s_exd, 1)
                if n % 2:
                    pool.wait_ge(s_exd, 2 * n + 2)
                    pool.sem_inc(s_exr, 8)

            halves = 2 * (NE - PRE)
            pool.wait_ge(s_pos, 1)
            pool.wait_ge(s_zero, 16 * (2 * NSX - FULL))
            for t in range(NT):
                scatter(t)
                if t == 3:
                    pool.wait_ge(s_wlo, 40)
                    expert_load(0)
                    expert_load(1)
            pool.sem_inc(s_exr, 8 * PRE)

            for n in range(halves):
                expert_split(n)
                if n + 2 < halves:
                    expert_load(n + 2)
                if n == 0:
                    pool.wait_ge(s_dn, NT)
                    for i in range(2):
                        pool.wait_ge(s_basest[i], 16 * NT // 2)
                if n < NT:
                    pool.dma_start(bsb[:, n], base_s[n]).then_inc(s_bsl, 16)
                elif n < NT + NB:
                    pool.dma_start(gb2[:, n - NT], mod_s[5, n - NT:n - NT + 1, :].partition_broadcast(P))\
                        .then_inc(s_bsl, 16)

            pool.wait_ge(s_end, 2)
            for t in range(NT):
                if t >= NG:
                    pool.wait_ge(s_out[t % NG], 16 * (NB + t // NG))
                for c, buf in ((0, g1b), (1, g2b)):
                    pool.indirect_dma_start(buf[:, t % NG], None, ys_s,
                                            bass.IndirectOffsetOnAxis(ap=pos[:, c, t:t + 1], axis=0))\
                        .then_inc(s_scat[t % NG], 16)


def kernel(**inputs):
    import numpy as np
    import concourse.bacc as bacc
    from concourse import mybir as mb
    from concourse.bass_utils import run_bass_kernel_spmd as run

    def tiled(w):
        k, n = w.shape
        return np.ascontiguousarray(w.reshape(k // 128, 128, n).transpose(1, 0, 2).reshape(128, -1))

    g = {k.removeprefix("L0_"): np.asarray(v) for k, v in inputs.items()}
    x = g["attn_x"].reshape(16, 128, 512)
    c = np.ascontiguousarray(g["c"].T.reshape(4, 128, 4).transpose(1, 0, 2))
    wmod = np.stack([tiled(g["wmod"][:, i * 512:(i + 1) * 512]).reshape(128, 4, 512) for i in range(6)])
    names = ["tm_mk", "tm_mv", "tm_mr", "cm_mk", "cm_mr", "ln1_g", "ln1_b", "ln2_g", "ln2_b", "tm_first"]
    vecs = np.ascontiguousarray(np.stack([g["attn_" + n].reshape(4, 128).T for n in names], axis=1))
    wtm = np.stack([tiled(g["attn_" + n].T) for n in ("Wk", "Wv", "Wr", "Wo", "Wcr")])
    wkey = g["attn_Wkey"].T
    wval = g["attn_Wval"].T
    wcm = np.stack([tiled(w) for j in range(4) for w in (wkey[:, j * 512:(j + 1) * 512], wval[j * 512:(j + 1) * 512])])
    up = [g["ffn_Wsh_up"].transpose(1, 0, 2).reshape(512, 512)]
    down = [g["ffn_Wsh_down"].reshape(512, 512)]
    wex = np.stack([tiled(up[0]), tiled(down[0])] +
                   [np.concatenate([tiled(g["ffn_Wrt_up"][e]), tiled(g["ffn_Wrt_down"][e])], axis=1) for e in range(16)])
    ins = {"x": x, "c": c, "wmod": wmod, "vecs": vecs, "wtm": wtm, "wcm": wcm,
           "wrt": tiled(g["ffn_W_router"]).reshape(128, 4, 16), "wex": wex}
    nc = bacc.Bacc("TRN2", target_bir_lowering=False, num_devices=1)
    arrays, args = {}, []
    for name, a in ins.items():
        a = np.ascontiguousarray(a)
        arrays[f"in_{name}"] = a
        args.append(nc.dram_tensor(f"in_{name}", a.shape, mb.dt.from_np(a.dtype), kind="ExternalInput").ap())
    out = nc.dram_tensor("out_0", (16, 128, 512), mb.dt.float32, kind="ExternalOutput").ap()
    adaln_block(nc, *args, out)
    r = run(nc, [arrays], core_ids=[0])
    return r.results[0]["out_0"].reshape(4, 512, 512)
```
